# Optimizing a Trainium2 kernel written in Bass

```python
import numpy as np
import jax
import jax.numpy as jnp

def _softmax(x, axis=-1):
    return jax.nn.softmax(x, axis=axis)

def _gelu(x):
    return jax.nn.gelu(x, approximate=True)

def _silu(x):
    return jax.nn.silu(x)

def _sigmoid(x):
    return jax.nn.sigmoid(x)

def _layernorm(x, axis=-1, eps=1e-05):
    m = jnp.mean(x, axis=axis, keepdims=True)
    v = jnp.var(x, axis=axis, keepdims=True)
    return (x - m) / jnp.sqrt(v + eps)

def _scatter_add(tgt, idx, src, axis=0):
    return tgt.at[idx].add(src)

def _segment_sum(src, seg, n):
    return jax.ops.segment_sum(src, seg, n)
kernel_name = 'mk_sandwich_d1_jaxref_r8_24f7d8'

def setup_inputs(seed: int=0):
    np.random.seed(seed)
    _w = jnp.asarray

    def _L0_attn_setup():
        import jax, jax.numpy as jnp
        import numpy as np
        DILATION_RATE = 4
        SEGMENT_SIZE = 64
        key = jax.random.key(seed)
        x = jax.random.normal(key, (4, 1024, 128), dtype=jnp.float32)
        return {'x': x}
    _L0_attn_in = _L0_attn_setup()

    def _L0_ffn_setup():
        import math
        import jax, jax.numpy as jnp
        import numpy as np
        B, T, D, H, E, K, S = (4, 512, 128, 256, 16, 2, 2)
        ROUTE_SCALE = 1.0

        def _swiglu(x, w1, w3, w2):
            return jax.nn.silu(x @ w1) * (x @ w3) @ w2
        key = jax.random.key(seed)
        ks = jax.random.split(key, 9)
        s = 0.02
        return {'x': jax.random.normal(ks[0], (B, T, D), jnp.float32), 'gate_w': jax.random.normal(ks[1], (D, E), jnp.float32) * s, 'gate_b': jnp.zeros((E,), jnp.float32), 'ew1': jax.random.normal(ks[2], (E, D, H), jnp.float32) * s, 'ew3': jax.random.normal(ks[3], (E, D, H), jnp.float32) * s, 'ew2': jax.random.normal(ks[4], (E, H, D), jnp.float32) * s, 'sw1': jax.random.normal(ks[5], (S, D, H), jnp.float32) * s, 'sw3': jax.random.normal(ks[6], (S, D, H), jnp.float32) * s, 'sw2': jax.random.normal(ks[7], (S, H, D), jnp.float32) * s}
    _L0_ffn_in = _L0_ffn_setup()
    _d = {'L0_attn_x': _L0_attn_in['x'], 'L0_ffn_gate_w': _L0_ffn_in['gate_w'], 'L0_ffn_gate_b': _L0_ffn_in['gate_b'], 'L0_ffn_ew1': _L0_ffn_in['ew1'], 'L0_ffn_ew3': _L0_ffn_in['ew3'], 'L0_ffn_ew2': _L0_ffn_in['ew2'], 'L0_ffn_sw1': _L0_ffn_in['sw1'], 'L0_ffn_sw3': _L0_ffn_in['sw3'], 'L0_ffn_sw2': _L0_ffn_in['sw2']}
    _x0 = _d['L0_attn_x']
    _d['L0_attn_x'] = jax.random.normal(jax.random.fold_in(jax.random.key(seed), 1), (4, 512, 128), dtype=_x0.dtype)
    del _x0
    return _d

def reference(L0_attn_x, L0_ffn_gate_w, L0_ffn_gate_b, L0_ffn_ew1, L0_ffn_ew3, L0_ffn_ew2, L0_ffn_sw1, L0_ffn_sw3, L0_ffn_sw2):

    def _L0_attn_ref(x):
        import jax, jax.numpy as jnp
        import numpy as np
        DILATION_RATE = 4
        SEGMENT_SIZE = 64
        'LongNet-style dilated attention.\n\n            For each offset in range(dilation_rate): take the strided slice\n            x[:, offset::r, :], split it into segments of length `segment_size`,\n            run full softmax(q k^T / sqrt(d)) v attention inside each segment\n            (q=k=v=the slice; attention dim is the full d_model, matching how the\n            original feeds [B, n_seg, seg, d_model] to FlashAttention), scatter the\n            result back to the strided positions, and average the dilation heads\n            (softmax over uniform logits == 1/r weights).\n\n            Since seq_len % (r * segment_size) == 0, the r strided slices tile the\n            sequence exactly, so we vectorize over offsets with a single reshape:\n            position p = i*r + offset  ->  xr[:, i, offset, :].\n            '
        r, seg = (DILATION_RATE, SEGMENT_SIZE)
        B, S, D = x.shape
        n = S // r
        g = n // seg
        scale = 1.0 / jnp.sqrt(jnp.asarray(D, dtype=x.dtype))
        xs = x.reshape(B, g, seg, r, D)
        scores = jnp.einsum('bgqrd,bgkrd->brgqk', xs, xs) * scale
        probs = jax.nn.softmax(scores, axis=-1)
        out = jnp.einsum('brgqk,bgkrd->bgqrd', probs, xs)
        return out.reshape(B, S, D) / r

    def _L0_ffn_ref(x, gate_w, gate_b, ew1, ew3, ew2, sw1, sw3, sw2):
        import math
        import jax, jax.numpy as jnp
        import numpy as np
        B, T, D, H, E, K, S = (4, 512, 128, 256, 16, 2, 2)
        ROUTE_SCALE = 1.0

        def _swiglu(x, w1, w3, w2):
            return jax.nn.silu(x @ w1) * (x @ w3) @ w2
        Bx, Tx, Dx = x.shape
        flat = x.reshape(-1, Dx)
        N = flat.shape[0]
        n_experts = gate_w.shape[1]
        logits = flat @ gate_w
        scores = jax.nn.softmax(logits.astype(jnp.float32), -1) + gate_b
        _, topi = jax.lax.top_k(scores, K)
        weights = jnp.take_along_axis(logits, topi, axis=-1) * ROUTE_SCALE
        weights = weights.astype(flat.dtype)
        capacity = math.ceil(N * K / n_experts * 1.25)

        def per_expert(gid, w1, w3, w2):
            match = topi == gid
            assigned = match.any(-1)
            w_tok = jnp.sum(jnp.where(match, weights, 0.0), -1)
            wm = jnp.where(assigned, w_tok, -jnp.inf)
            vals, idx = jax.lax.top_k(wm, capacity)
            valid = assigned[idx]
            xs = flat[idx]
            y = _swiglu(xs, w1, w3, w2) * jnp.where(valid, vals, 0.0)[:, None]
            return (idx, y)
        idxs, ys = jax.vmap(per_expert)(jnp.arange(n_experts), ew1, ew3, ew2)
        out = jnp.zeros_like(flat).at[idxs.reshape(-1)].add(ys.reshape(-1, Dx))
        shared = jax.vmap(lambda w1, w3, w2: _swiglu(flat, w1, w3, w2))(sw1, sw3, sw2)
        out = out + shared.mean(0)
        return out.reshape(Bx, Tx, Dx)
    x = L0_attn_x
    x = x + _layernorm(_L0_attn_ref(_layernorm(x, axis=-1)), axis=-1)
    x = x + _layernorm(_L0_ffn_ref(_layernorm(x, axis=-1), L0_ffn_gate_w, L0_ffn_gate_b, L0_ffn_ew1, L0_ffn_ew3, L0_ffn_ew2, L0_ffn_sw1, L0_ffn_sw3, L0_ffn_sw2), axis=-1)
    return x

_drawn_inputs = setup_inputs


def setup_inputs(seed=0):
    import zlib

    import numpy as np

    out = dict(_drawn_inputs(seed))
    spreads = {'L0_ffn_gate_b': (0.0, 0.1)}
    factors = {}
    for name, (base, spread) in spreads.items():
        noise = np.random.default_rng([zlib.crc32(name.encode()), seed]).standard_normal(out[name].shape)
        drawn = base * np.exp(spread * noise) if base else spread * noise
        out[name] = jnp.asarray(drawn.astype(out[name].dtype))
    for name, factor in factors.items():
        out[name] = (out[name] * factor).astype(out[name].dtype)
    return out
```

```python
from contextlib import ExitStack

import concourse.bass as bass
import numpy as np
from concourse import mybir

B, T, D, E, H, S = 4, 512, 128, 16, 256, 2
N = B * T
NT = N // 128
CAP = 320
CH = 8
CW = N // CH
HB = H // 128
SLOT_ROWS = (128, 128, 64)
HW = 132
EPS = 1e-5
UNASSIGNED = -3.0e38
ROUNDS = 8

C_ID, C_BLOCK, C_BEFORE, C_DELTA = 0, 128, 256, 384
C_IOTA = 512
C_CAND = C_IOTA + 384
C_STEP = C_CAND + 3 * ROUNDS
C_REV = C_STEP + ROUNDS
C_EIX = C_REV + E
C_SLOT = C_EIX + E
C_GBASE = C_SLOT + 3
C_CBASE = C_GBASE + 1
C_HALF = C_CBASE + 1
C_JIX = C_HALF + NT
C_PAD = C_JIX + E * E
C_ALL = C_PAD + HW


def constants():
    c = np.zeros((128, C_ALL), np.float32)
    p = np.arange(128)
    c[:, C_ID:C_ID + 128] = np.eye(128)
    same = p[:, None] // CH == p[None, :] // CH
    c[:, C_BLOCK:C_BLOCK + 128] = same
    c[:, C_BEFORE:C_BEFORE + 128] = same & (p[:, None] < p[None, :])
    c[:, C_DELTA:C_DELTA + 128] = np.eye(128) - np.eye(128, k=1)
    c[:, C_IOTA:C_IOTA + 384] = np.arange(384)
    for k in range(ROUNDS):
        step = 4 ** (ROUNDS - 1 - k)
        c[:, C_CAND + 3 * k:C_CAND + 3 * k + 3] = step * np.arange(1, 4)
        c[:, C_STEP + k] = step
    c[:, C_REV:C_REV + E] = E - np.arange(E)
    c[:, C_EIX:C_EIX + E] = np.arange(E)
    for k in range(3):
        c[:, C_SLOT + k] = p + 128 * k
    c[:, C_GBASE] = CAP * (p // CH)
    c[:, C_CBASE] = CW * (p % CH)
    c[:, C_HALF:C_HALF + NT] = -0.5
    c[:, C_JIX:C_JIX + E * E] = np.repeat(np.arange(E), E)
    c[:, C_PAD + D] = -1.0
    return c


def build(nc, x, gate_w, gate_b, ew1, ew3, ew2, sw1, sw3, sw2, consts, out):
    f32, bf16, f16, i32 = mybir.dt.float32, mybir.dt.bfloat16, mybir.dt.float16, mybir.dt.int32
    ALU, ACT, AX = mybir.AluOpType, mybir.ActivationFunctionType, mybir.AxisListType.X
    v, s_, g_ = nc.vector, nc.scalar, nc.gpsimd

    ctx = ExitStack()
    with ctx:
        def sb(name, shape, dt=f32):
            return ctx.enter_context(nc.sbuf_tensor(name, shape, dt))

        def sem(name):
            return ctx.enter_context(nc.semaphore(name))

        htab = nc.dram_tensor("htab", [N + 1, HW], f32).ap()
        ytab = nc.dram_tensor("ytab", [2 * N, D], f32).ap()

        def tiled(ap):
            v = ap.rearrange("(a q rp r2) d -> r2 rp q a d", q=64, rp=2, r2=2)
            return [[v[r2][rp] for rp in range(2)] for r2 in range(2)]

        def tiles(buf):
            v = buf[:, :, :].rearrange("p (a rp) d -> p rp a d", rp=2)
            return [[v[64 * r2:64 * r2 + 64, rp] for rp in range(2)] for r2 in range(2)]

        def move(eng, dst, src, done):
            for r2 in range(2):
                for rp in range(2):
                    eng.dma_start(dst[r2][rp], src[r2][rp]).then_inc(done, 16)

        def less_one(i, top):
            return (i * (top - 1)) >> (top.bit_length() - 1)

        cst = sb("cst", [128, C_ALL])
        xs_in = sb("x_in", [128, NT, D])
        xn = sb("xn", [128, NT, D])
        xnT = sb("xnT", [128, NT, 128])
        P = sb("P", [128, NT, 128])
        x1 = sb("x1", [128, NT, D])
        h = sb("h", [128, NT, HW])
        hT = sb("hT", [128, NT * 128])
        ones = sb("ones", [128, 2])
        zeros = sb("zeros", [128, 2048])
        bn = sb("bn", [128, NT, 6])
        mv = sb("mv", [128, NT, 2])
        var = sb("var", [128, NT])
        lsum = sb("lsum", [128, NT])
        rstd = sb("rstd", [128, NT])
        lg = sb("lg", [128, NT, E])
        mx = sb("mx", [128, NT])
        ex = sb("ex", [128, NT, E])
        sc = sb("sc", [128, NT, E])
        tA = sb("tA", [128, NT, E])
        oh1 = sb("oh1", [128, NT, E])
        oh2 = sb("oh2", [128, NT, E])
        asg = sb("asg", [128, NT, E], bf16)
        first = sb("first", [128, NT])
        second = sb("second", [128, NT])
        w_1 = sb("w_1", [128, NT])
        w_2 = sb("w_2", [128, NT])
        bias = sb("bias", [128, E])
        gw = sb("gw", [128, E])
        wmP = sb("wmP", [128, NT, 128])
        onesb = sb("onesb", [128, 128], bf16)
        blockb = sb("blockb", [128, 128], bf16)
        beforef = cst[:, C_BEFORE:C_BEFORE + 128]
        deltah = sb("deltah", [128, 128], f16)
        ident = cst[:, C_ID:C_ID + 128]
        act = sb("act", [128, E])
        rank = sb("rank", [128, E])
        hit = sb("hit", [128, E, E])
        elist = sb("elist", [128, E])
        e320 = sb("e320", [128, E])
        elist_i = sb("elist_i", [128, E + 1], i32)
        K = sb("K", [128, CW])
        m32 = sb("m32", [128, CW], i32)
        u32 = sb("u32", [128, CW], i32)
        part = sb("part", [128, CW], i32)
        hi = sb("hi", [128, CW])
        lo = sb("lo", [128, CW])
        key2 = sb("key2", [128, CW])
        assigned = sb("assigned", [128, CW])
        junk = sb("junk", [128, 3, CW])
        above = sb("above", [128, CW])
        base = sb("base", [128, 1])
        hbase = sb("hbase", [128, 1])
        cand = sb("cand", [128, 3])
        cnt = sb("cnt", [128, 3], bf16)
        dec3 = sb("dec3", [128, 3])
        dec = sb("dec", [128, 1])
        tot = sb("tot", [128, 2])
        eqm = sb("eqm", [128, CW])
        eqs = sb("eqs", [128, CW])
        sel = sb("sel", [128, CW])
        selp = sb("selp", [128, CW])
        rem = sb("rem", [128, 1])
        off = sb("off", [128, 1])
        gstart = sb("gstart", [128, 1])
        R = sb("R", [128, CW + 1], f16)
        Dl = sb("Dl", [128, CW + 1], f16)
        w1s = sb("w1s", [128, S, H])
        w3s = sb("w3s", [128, S, H])
        w2s = sb("w2s", [128, S * HB, D])
        sil = sb("sil", [128, 2, 512])
        gu = sb("gu", [128, S * HB, 512])
        shared = sb("shared", [128, NT, D])
        ge = sb("ge", [128, 2, 384], f16)
        tokc = sb("tokc", [128, 2, 3])
        tokf = sb("tokf", [128, E * 3])
        toki = sb("toki", [128, E * 3], i32)
        idx = sb("idx", [128, 2, 3], i32)
        ne1 = sb("ne1", [128, 2, 3])
        dst = sb("dst", [128, 2, 3], i32)
        xg = sb("xg", [128, 2, 3, HW])
        xgT = sb("xgT", [128, 2, CAP])
        w1e = sb("w1e", [128, 2, H])
        w3e = sb("w3e", [128, 2, H])
        w2e = sb("w2e", [128, 2, HB, D])
        sile = sb("sile", [128, HB, CAP])
        gue = sb("gue", [128, HB, CAP])
        ye = sb("ye", [128, 2, 3, D])
        y1 = sb("y1", [128, NT, D])
        y2 = sb("y2", [128, NT, D])
        res = sb("res", [128, NT, D])

        bank = [ctx.enter_context(nc.psum_tensor(f"bank{i}", [128, 512], f32)) for i in range(8)]

        s_const, s_x, s_w, s_bias = sem("const_loaded"), sem("x_loaded"), sem("weights_loaded"), sem("bias_loaded")
        s_zero, s_yz, s_pad, s_hw = sem("zeros_set"), sem("ytab_zeroed"), sem("pad_row_written"), sem("htab_written")
        s_ln1, s_ln2, s_ln3, s_ln4 = sem("var1_ready"), sem("var2_ready"), sem("var3_ready"), sem("var4_ready")
        s_pw = sem("rstd_ready")
        s_xn, s_xt, s_xtc = sem("xn_ready"), sem("x_transposed"), sem("xT_copied")
        s_sc, s_ex, s_pv, s_pvu = sem("scores_ready"), sem("probs_ready"), sem("attn_ready"), sem("attn_used")
        s_h, s_ht, s_htc, s_lg = sem("h_ready"), sem("h_transposed"), sem("hT_copied"), sem("logits_ready")
        s_lmx, s_gex = sem("logits_centred"), sem("gate_exp_ready")
        s_h1 = sem("first_choice_in_h")
        s_asg, s_nct = sem("assigned_ready"), sem("expert_counts_ready")
        s_list = sem("list_ready")
        s_wm, s_kt = sem("masked_logits_ready"), sem("expert_major_ready")
        s_kc = sem("expert_major_copied")
        s_cnt, s_tot = sem("counts_ready"), sem("totals_ready")
        s_up, s_sil, s_gu, s_dn, s_shc = (sem("shared_up_done"), sem("shared_silu_done"), sem("shared_gu_done"),
                                          sem("shared_down_done"), sem("shared_copied"))
        s_eq, s_eqt, s_sl, s_slt, s_R, s_D, s_Dc = (sem("ties_counted"), sem("tie_totals"), sem("selected_counted"),
                                              sem("selected_totals"), sem("rows_ready"), sem("differences_ready"),
                                              sem("differences_copied"))
        s_ge, s_G, s_tok, s_Gu = sem("slots_compared"), sem("prefix_rows_ready"), sem("tokens_of_slots"), sem("prefix_rows_used")
        s_wl = [sem("expert_weights_even"), sem("expert_weights_odd")]
        s_gat = [sem("rows_gathered_even"), sem("rows_gathered_odd")]
        s_sct = [sem("rows_scattered_even"), sem("rows_scattered_odd")]
        s_idx, s_dst = sem("index_copied"), sem("destinations_ready")
        s_gt, s_gtc = sem("gathered_transposed"), sem("gathered_T_copied")
        s_eu, s_es, s_eg, s_ed, s_yc = (sem("expert_up_done"), sem("expert_silu_done"), sem("expert_gu_done"),
                                        sem("expert_down_done"), sem("expert_out_copied"))
        s_yl, s_fin, s_out = sem("y_loaded"), sem("result_ready"), sem("out_written")
        s_v, s_a, s_p = sem("vector_step"), sem("scalar_step"), sem("pool_step")

        block = ctx.enter_context(nc.Block())

        def of_slot(ap, j):
            return ap[:, bass.ds(j, 1)]

        @block.sync
        def _(sp):
            sp.dma_start(cst[:], consts).then_inc(s_const, 16)
            move(sp, tiles(xs_in), tiled(x), s_x)
            sp.dma_start(gw[:], gate_w).then_inc(s_w, 16)
            sp.dma_start(w1s[:], sw1.rearrange("s d h -> d s h")).then_inc(s_w, 16)
            sp.dma_start(w3s[:], sw3.rearrange("s d h -> d s h")).then_inc(s_w, 16)
            sp.dma_start(w2s[:], sw2.rearrange("s (k p) d -> p (s k) d", p=128)).then_inc(s_w, 16)
            sp.dma_start(bias[:], gate_b.rearrange("(o e) -> o e", o=1).broadcast_to([128, E])).then_inc(s_bias, 16)
            sp.wait_ge(s_zero, 1)
            for k in range(2):
                sp.dma_start(ytab[N * k:N * (k + 1), :].rearrange("(p r) d -> p (r d)", p=128),
                             zeros[:, :]).then_inc(s_yz, 16)
            sp.wait_ge(s_const, 16)
            sp.dma_start(htab[N:N + 1, :], cst[0:1, C_PAD:C_PAD + HW]).then_inc(s_pad, 16)
            sp.wait_ge(s_h1, 1)
            move(sp, tiled(htab[0:N, :]), tiles(h), s_hw)
            sp.wait_ge(s_list, 1)
            n = sp.value_load(elist_i[0:1, E:E + 1], min_val=2, max_val=E)
            with sp.Fori(0, E - 1, 2) as i:
                for k in range(2):
                    with sp.If(i + k < n):
                        e = sp.value_load(elist_i[0:1, bass.ds(i + k, 1)], min_val=0, max_val=E - 1)
                        sp.wait_ge(s_ed, less_one(i, E) if k == 0 else i)
                        sp.dma_start(w1e[:, k], ew1[bass.ds(e, 1)].rearrange("o d h -> d (o h)")).then_inc(s_wl[k], 16)
                        sp.dma_start(w3e[:, k], ew3[bass.ds(e, 1)].rearrange("o d h -> d (o h)")).then_inc(s_wl[k], 16)
                        sp.dma_start(w2e[:, k], ew2[bass.ds(e, 1)].rearrange("o (k p) d -> p (o k) d", p=128)).then_inc(s_wl[k], 16)
            sp.wait_ge(s_sct[0], 48 * ((n + 1) // 2))
            sp.wait_ge(s_sct[1], 48 * (n // 2))
            for k, y in enumerate((y1, y2)):
                move(sp, tiles(y), tiled(ytab[N * k:N * (k + 1), :]), s_yl)
            sp.wait_ge(s_fin, 1)
            move(sp, tiled(out), tiles(res), s_out)
            sp.wait_ge(s_out, 64)

        @block.gpsimd
        def _(pool):
            done = [0]

            def link(ins):
                done[0] += 1
                ins.then_inc(s_p, 1)
                pool.wait_ge(s_p, done[0])

            g_.memset(zeros[:], 0.0).then_inc(s_zero, 1)
            g_.memset(wmP[:], 0.0)
            g_.memset(onesb[:], 1.0)
            g_.memset(ones[:], 1.0)
            g_.memset(xg[:], 0.0)
            g_.memset(tokc[:], 0.0)
            link(g_.memset(P[:], 0.0))
            s = s_const
            pool.wait_ge(s, 16)
            g_.tensor_copy(blockb[:], cst[:, C_BLOCK:C_BLOCK + 128])
            link(g_.tensor_copy(deltah[:], cst[:, C_DELTA:C_DELTA + 128]))
            for k, ready in enumerate((s_ln1, s_ln2, s_ln3)):
                pool.wait_ge(ready, 1)
                g_.tensor_tensor(rstd[:], var[:], cst[:, C_HALF:C_HALF + NT], ALU.pow).then_inc(s_pw, 1)
            pool.wait_ge(s_pad, 16)
            pool.wait_ge(s_list, 1)
            n = pool.value_load(elist_i[0:1, E:E + 1], min_val=2, max_val=E)

            last_token, last_result = pool.to_reg(N), pool.to_reg(2 * N - 1)

            def gather(j, k, nth):
                pool.wait_ge(s_tok, j + 1)
                g_.tensor_copy(idx[:, k], toki[:, bass.ds(3 * j, 3)]).then_inc(s_idx, 1)
                pool.wait_ge(s_hw, 64)
                pool.wait_ge(s_idx, j + 1)
                for m, rows in enumerate(SLOT_ROWS):
                    g_.indirect_dma_start(
                        out=xg[0:rows, k, m, :], out_offset=None, in_=htab[:, :],
                        in_offset=bass.IndirectOffsetOnAxis(ap=idx[0:rows, k, m:m + 1], axis=0),
                        bounds_check=last_token, oob_is_err=False).then_inc(s_gat[k], 16)

            with pool.Fori(0, E - 1, 2) as i:
                for k in range(2):
                    with pool.If(i + k < n):
                        pool.wait_ge(s_gt, less_one(i, E) if k == 0 else i)
                        pool.wait_ge(s_dst, less_one(i, E) if k == 0 else i)
                        gather(i + k, k, i)
                        pool.wait_ge(s_yz, 32)
                        pool.wait_ge(s_dst, i + k + 1)
                        pool.wait_ge(s_yc, i + k + 1)
                        for m, rows in enumerate(SLOT_ROWS):
                            g_.indirect_dma_start(
                                out=ytab[:, :], out_offset=bass.IndirectOffsetOnAxis(ap=dst[0:rows, k, m:m + 1], axis=0),
                                in_=ye[0:rows, k, m, :], in_offset=None,
                                bounds_check=last_result, oob_is_err=False).then_inc(s_sct[k], 16)
            pool.wait_ge(s_ln4, 1)
            g_.tensor_tensor(rstd[:], var[:], cst[:, C_HALF:C_HALF + NT], ALU.pow).then_inc(s_pw, 1)

        @block.scalar
        def _(ac):
            for b in range(B):
                t = 4 * b
                ac.wait_ge(s_xt, b + 1)
                s_.copy(xnT[:, t:t + 4, :], bank[b % 2][:, :]).then_inc(s_xtc, 1)
                ac.wait_ge(s_sc, b + 1)
                if b == 0:
                    ac.wait_ge(s_p, 1)
                sc4 = bank[2 + b % 2][:, :].rearrange("p (t k) -> p t k", t=4)
                for r2 in range(2):
                    q = slice(64 * r2, 64 * r2 + 64)
                    s_.activation(P[q, t:t + 4, q], sc4[q, :, q], ACT.Exp, scale=float(D) ** -0.5).then_inc(s_ex, 1)
            for b in range(B):
                ac.wait_ge(s_ht, b + 1)
                s_.copy(hT[:, 512 * b:512 * b + 512], bank[b % 2][:, :]).then_inc(s_htc, 1)
            ac.wait_ge(s_lmx, 1)
            s_.activation(ex[:], sc[:], ACT.Exp).then_inc(s_gex, 1)
            with ac.Fori(0, 4) as c:
                for k in range(S * HB):
                    ac.wait_ge(s_up, c * 4 + k + 1)
                    ac.wait_ge(s_gu, 4 * c + k - 1 if k else less_one(4 * c, 16))
                    s_.activation(sil[:, k % 2], bank[k % 2][:], ACT.Silu).then_inc(s_sil, 1)
                ac.wait_ge(s_dn, c + 1)
                s_.copy(shared[:, bass.ds(4 * c, 4), :], bank[4][:]).then_inc(s_shc, 1)
            n = ac.value_load(elist_i[0:1, E:E + 1], min_val=2, max_val=E)
            with ac.Fori(0, E - 1, 2) as i:
                for k in range(2):
                    with ac.If(i + k < n):
                        ac.wait_ge(s_gt, i + k + 1)
                        s_.copy(xgT[:, k], bank[0][:, 0:CAP]).then_inc(s_gtc, 1)
                        for hb in range(HB):
                            ac.wait_ge(s_eu, 2 * (i + k) + hb + 1)
                            s_.activation(sile[:, hb], bank[1 + hb][:, 0:CAP], ACT.Silu).then_inc(s_es, 1)
                        ac.wait_ge(s_ed, i + k + 1)
                        ac.wait_ge(s_sct[k], 24 * i)
                        s_.copy(ye[:, k, 0:2], bank[5][:, 0:256])
                        s_.copy(ye[0:64, k, 2], bank[5][0:64, 256:384]).then_inc(s_yc, 1)

        @block.vector
        def _(dv):
            done = [0, 0]

            def link(ins):
                done[0] += 1
                ins.then_inc(s_v, 1)
                dv.wait_ge(s_v, done[0] + done[1])

            def stats(src, ready, extra=None):
                for t in range(NT):
                    last = v.bn_stats(bn[:, t, :], src(t))
                link(last)
                for t in range(NT):
                    last = v.bn_aggr(mv[:, t, :], bn[:, t, :])
                link(last)

            def bc(ap):
                return ap[:, :].rearrange("p (t o) -> p t o", o=1).broadcast_to([128, NT, E])

            dv.wait_ge(s_x, 64)
            stats(lambda t: xs_in[:, t, :], s_ln1)
            v.tensor_scalar(var[:], mv[:, :, 1], EPS, None, ALU.add).then_inc(s_ln1, 1)
            dv.wait_ge(s_pw, 1)
            for t in range(NT):
                last = v.tensor_scalar(xn[:, t, :], xs_in[:, t, :], mv[:, t, 0:1], rstd[:, t:t + 1],
                                       ALU.subtract, ALU.mult)
                if t % 4 == 3:
                    last.then_inc(s_xn, 1)
            for b in range(B):
                dv.wait_ge(s_pv, b + 1)
                o = bank[4 + b % 2]
                for t in range(4 * b, 4 * b + 4):
                    v.bn_stats(bn[:, t, :], o[:, 128 * (t % 4):128 * (t % 4) + 128])
                v.tensor_copy(x1[:, 4 * b:4 * b + 4, :], o[:, :])
                link(v.tensor_copy(lsum[:, 4 * b:4 * b + 4],
                                   bank[6 + b % 2][:, 0:8].rearrange("p (t w) -> p t w", w=2)[:, :, 0]))
                for t in range(4 * b, 4 * b + 4):
                    last = v.bn_aggr(mv[:, t, :], bn[:, t, :])
                last.then_inc(s_pvu, 1)
            dv.wait_ge(s_pvu, B)
            link(v.scalar_tensor_tensor(mx[:], lsum[:], EPS * 16, lsum[:], ALU.mult, ALU.mult))
            v.tensor_tensor(var[:], mx[:], mv[:, :, 1], ALU.add).then_inc(s_ln2, 1)
            dv.wait_ge(s_pw, 2)
            for t in range(NT):
                last = v.tensor_scalar(x1[:, t, :], x1[:, t, :], mv[:, t, 0:1], rstd[:, t:t + 1],
                                       ALU.subtract, ALU.mult)
            link(last)
            link(v.tensor_tensor(x1[:], x1[:], xs_in[:], ALU.add))
            stats(lambda t: x1[:, t, :], s_ln3)
            v.tensor_scalar(var[:], mv[:, :, 1], EPS, None, ALU.add).then_inc(s_ln3, 1)
            dv.wait_ge(s_pw, 3)
            for t in range(NT):
                last = v.tensor_scalar(h[:, t, 0:D], x1[:, t, :], mv[:, t, 0:1], rstd[:, t:t + 1],
                                       ALU.subtract, ALU.mult)
                if t % 4 == 3:
                    last.then_inc(s_h, 1)
            dv.wait_ge(s_lg, 1)
            link(v.tensor_copy(lg[:], bank[6][:, 256:512]))
            link(v.tensor_reduce(mx[:], lg[:], AX, ALU.max))
            v.tensor_tensor(sc[:], lg[:], bc(mx), ALU.subtract).then_inc(s_lmx, 1)
            dv.wait_ge(s_gex, 1)
            link(v.tensor_reduce(mx[:], ex[:], AX, ALU.add))
            link(v.reciprocal(first[:], mx[:]))
            link(v.tensor_tensor(sc[:], ex[:], bc(first), ALU.mult))
            dv.wait_ge(s_bias, 16)
            link(v.tensor_tensor(sc[:], sc[:], bias[:, :].rearrange("p (o e) -> p o e", o=1).broadcast_to([128, NT, E]), ALU.add))
            rev = cst[:, C_REV:C_REV + E].rearrange("p (o e) -> p o e", o=1).broadcast_to([128, NT, E])

            def best(oh, pick):
                link(v.tensor_reduce(mx[:], sc[:], AX, ALU.max))
                link(v.tensor_tensor(tA[:], sc[:], bc(mx), ALU.is_equal))
                link(v.tensor_tensor(tA[:], tA[:], rev, ALU.mult))
                link(v.tensor_reduce(pick[:], tA[:], AX, ALU.max))
                link(v.tensor_tensor(oh[:], rev, bc(pick), ALU.is_equal))

            best(oh1, first)
            v.tensor_scalar(h[:, :, D:HW], first[:, :].rearrange("p (t o) -> p t o", o=1).broadcast_to([128, NT, HW - D]),
                            -1.0, float(E), ALU.mult, ALU.add).then_inc(s_h1, 1)
            link(v.scalar_tensor_tensor(sc[:], oh1[:], -1.0e30, sc[:], ALU.mult, ALU.add))
            best(oh2, second)
            v.tensor_tensor(asg[:], oh1[:], oh2[:], ALU.add).then_inc(s_asg, 1)
            v.tensor_tensor(oh1[:], oh1[:], lg[:], ALU.mult)
            dv.wait_ge(s_asg, 1)
            link(v.tensor_tensor(oh2[:], oh2[:], lg[:], ALU.mult))
            v.tensor_reduce(w_1[:], oh1[:], AX, ALU.add)
            v.tensor_reduce(w_2[:], oh2[:], AX, ALU.add)
            v.tensor_tensor(ex[:], oh1[:], oh2[:], ALU.add)
            link(v.tensor_scalar(tA[:], asg[:], -1.0, -UNASSIGNED, ALU.add, ALU.mult))
            for c in range(CH):
                last = v.tensor_tensor(wmP[:, 2 * c:2 * c + 2, :].rearrange("p t (e c) -> p t e c", c=CH)[:, :, :, c],
                                       tA[:, 2 * c:2 * c + 2, :], ex[:, 2 * c:2 * c + 2, :], ALU.add)
            last.then_inc(s_wm, 1)
            dv.wait_ge(s_nct, 1)
            link(v.tensor_reduce(act[:], bank[6][:, 0:256].rearrange("p (t e) -> p e t", e=E), AX, ALU.add))
            link(v.tensor_scalar(act[:], act[:], 1.0, None, ALU.min))
            link(v.tensor_tensor_scan(rank[:], ones[:, 0:1].broadcast_to([128, E]), act[:], 0.0, ALU.mult, ALU.add))
            link(v.tensor_scalar(mx[:], rank[:], -1.0, None, ALU.add))
            link(v.tensor_tensor(hit[:], cst[:, C_JIX:C_JIX + E * E].rearrange("p (j e) -> p j e", e=E),
                                 mx[:, :].rearrange("p (o e) -> p o e", o=1).broadcast_to([128, E, E]), ALU.is_equal))
            link(v.tensor_tensor(mx[:], act[:], cst[:, C_EIX:C_EIX + E], ALU.mult))
            link(v.tensor_tensor(hit[:], hit[:], mx[:, :].rearrange("p (o e) -> p o e", o=1).broadcast_to([128, E, E]), ALU.mult))
            link(v.tensor_reduce(elist[:], hit[:], AX, ALU.add))
            link(v.tensor_scalar(e320[:], elist[:], float(CAP), None, ALU.mult))
            v.tensor_copy(elist_i[:, E:E + 1], rank[:, E - 1:E])
            v.tensor_copy(elist_i[:, 0:E], elist[:]).then_inc(s_list, 1)
            dv.wait_ge(s_kt, 1)
            link(v.tensor_scalar(K[:, :].rearrange("p (q rp r2) -> p rp r2 q", rp=2, r2=2),
                                 bank[7][:, 0:CW].rearrange("p (rp r2 q) -> p rp r2 q", rp=2, r2=2), 0.0, None, ALU.add))
            v.tensor_scalar(assigned[:], K[:], UNASSIGNED / 2, None, ALU.is_gt)
            link(v.tensor_scalar(m32[:], K[:, :].bitcast(i32), 31, -2147483648, ALU.arith_shift_right, ALU.bitwise_or))
            link(v.tensor_tensor(u32[:], K[:, :].bitcast(i32), m32[:], ALU.bitwise_xor))
            link(v.tensor_scalar(part[:], u32[:], 16, None, ALU.logical_shift_right))
            link(v.tensor_copy(hi[:], part[:]))
            link(v.tensor_scalar(part[:], u32[:], 65535, None, ALU.bitwise_and))
            v.tensor_scalar(lo[:], part[:], 1.0, None, ALU.add)
            link(v.memset(base[:], 0.0))

            def shared_gu(c, k):
                dv.wait_ge(s_sil, c * 4 + k + 1)
                if k == 0:
                    dv.wait_ge(s_dn, c)
                v.scalar_tensor_tensor(gu[:, k], sil[:, k % 2], 1.0 / S, bank[2 + k % 2][:],
                                       ALU.mult, ALU.mult).then_inc(s_gu, 1)

            per_round = 3
            start = done[0]
            for half, key in enumerate((hi, key2)):
                with dv.Fori(0, 2) as i:
                    for k in range(4):
                        nth = i * 4 + k
                        steps = start + (half * ROUNDS + nth) * per_round + half * 5
                        v.tensor_scalar(cand[:], cst[:, bass.ds(C_CAND + 3 * nth, 3)], base[:, 0:1], None, ALU.add).then_inc(s_v, 1)
                        dv.wait_ge(s_v, steps + 1)
                        for m in range(3):
                            last = v.tensor_scalar(junk[:, m], key[:], cand[:, m:m + 1], None, ALU.is_ge, ALU.add,
                                                   accum_out=cnt[:, m:m + 1])
                        last.then_inc(s_cnt, 1)
                        shared_gu(half * 2 + i, k)
                        dv.wait_ge(s_tot, half * ROUNDS + nth + 1)
                        v.tensor_scalar(dec3[:], bank[6][:, 0:3], float(CAP), None, ALU.is_ge, ALU.add,
                                        accum_out=dec[:, 0:1]).then_inc(s_v, 1)
                        dv.wait_ge(s_v, steps + 2)
                        v.scalar_tensor_tensor(base[:], dec[:], cst[:, bass.ds(C_STEP + nth, 1)], base[:],
                                               ALU.mult, ALU.add).then_inc(s_v, 1)
                        dv.wait_ge(s_v, steps + 3)
                done[0] += ROUNDS * per_round
                if half == 0:
                    link(v.tensor_copy(hbase[:], base[:]))
                    link(v.memset(base[:], 1.0))
                    link(v.tensor_scalar(above[:], hi[:], hbase[:, 0:1], 65537.0, ALU.is_gt, ALU.mult))
                    link(v.scalar_tensor_tensor(key2[:], hi[:], hbase[:, 0:1], lo[:], ALU.is_equal, ALU.mult))
                    link(v.tensor_tensor(key2[:], key2[:], above[:], ALU.add))
            v.tensor_scalar(above[:], key2[:], base[:, 0:1], None, ALU.is_gt, ALU.add, accum_out=tot[:, 0:1])
            link(v.scalar_tensor_tensor(eqm[:], key2[:], base[:, 0:1], assigned[:], ALU.is_equal, ALU.mult))
            one = ones[:, 0:1].broadcast_to([128, CW])
            link(v.tensor_tensor_scan(eqs[:], one, eqm[:], 0.0, ALU.mult, ALU.add))
            v.tensor_copy(tot[:, 1:2], eqs[:, CW - 1:CW]).then_inc(s_eq, 1)
            dv.wait_ge(s_eqt, 1)
            link(v.tensor_scalar(rem[:], bank[6][:, 0:1], -1.0, float(CAP), ALU.mult, ALU.add))
            link(v.tensor_tensor(rem[:], rem[:], bank[6][:, 3:4], ALU.subtract))
            link(v.scalar_tensor_tensor(eqs[:], eqs[:], rem[:, 0:1], eqm[:], ALU.is_le, ALU.mult))
            link(v.tensor_tensor(sel[:], eqs[:], above[:], ALU.add))
            link(v.tensor_tensor_scan(selp[:], one, sel[:], 0.0, ALU.mult, ALU.add))
            v.tensor_copy(tot[:, 0:1], selp[:, CW - 1:CW]).then_inc(s_sl, 1)
            dv.wait_ge(s_slt, 1)
            link(v.tensor_copy(off[:], bank[6][:, 0:1]))
            v.tensor_copy(R[:, CW:CW + 1], cst[:, C_CBASE:C_CBASE + 1])
            v.tensor_tensor(gstart[:], off[:], cst[:, C_GBASE:C_GBASE + 1], ALU.add)
            v.tensor_scalar(R[:, 0:CW], selp[:], off[:, 0:1], None, ALU.add).then_inc(s_R, 1)
            dv.wait_ge(s_D, 1)
            v.tensor_copy(Dl[:], bank[7][:, 0:CW + 1]).then_inc(s_Dc, 1)
            n = dv.value_load(elist_i[0:1, E:E + 1], min_val=2, max_val=E)
            steps = done[0]
            dv.wait_ge(s_v, steps)
            dv.wait_ge(s_Dc, 1)
            with dv.Fori(0, E) as j:
                with dv.If(j < n):
                    v.tensor_scalar(ge[:, 0], cst[:, C_IOTA:C_IOTA + 384], of_slot(e320, j), gstart[:, 0:1],
                                    ALU.add, ALU.is_ge).then_inc(s_ge, 1)
                    dv.wait_ge(s_G, j + 1)
                    for m in range(3):
                        last = v.tensor_scalar(junk[:, m], bank[m][:, 0:CW], cst[:, C_SLOT + m:C_SLOT + m + 1], None,
                                               ALU.is_le, ALU.add, accum_out=tokc[:, 0, m:m + 1])
                    last.then_inc(s_v, 1)
                    dv.wait_ge(s_v, steps + 3 * j + 1)
                    for m in range(3):
                        last = v.tensor_tensor(tokf[:, bass.ds(3 * j + m, 1)], tokc[:, 0, m:m + 1],
                                               bank[m][:, CW:CW + 1], ALU.add)
                    last.then_inc(s_v, 2)
                    dv.wait_ge(s_v, steps + 3 * j + 3)
                    v.tensor_copy(toki[:, bass.ds(3 * j, 3)], tokf[:, bass.ds(3 * j, 3)]).then_inc(s_tok, 1)
            with dv.Fori(0, E - 1, 2) as i:
                for k in range(2):
                    with dv.If(i + k < n):
                        j = i + k
                        dv.wait_ge(s_gat[k], 24 * i + 48)
                        v.tensor_scalar(ne1[:, k], xg[:, k, :, D], of_slot(elist, j), float(N),
                                        ALU.not_equal, ALU.mult).then_inc(s_v, 1)
                        dv.wait_ge(s_v, steps + 3 * n + j + 1)
                        dv.wait_ge(s_sct[k], 24 * i)
                        v.tensor_tensor(dst[:, k], ne1[:, k], tokf[:, bass.ds(3 * j, 3)], ALU.add).then_inc(s_dst, 1)
                        for hb in range(HB):
                            dv.wait_ge(s_es, 2 * j + hb + 1)
                            v.tensor_tensor(gue[:, hb], sile[:, hb], bank[3 + hb][:, 0:CAP], ALU.mult).then_inc(s_eg, 1)
            dv.wait_ge(s_yl, 128)
            dv.wait_ge(s_shc, 4)

            def bd(ap, t):
                return ap[:, t:t + 1]

            for t in range(NT):
                last = v.scalar_tensor_tensor(y1[:, t, :], y1[:, t, :], bd(w_1, t), shared[:, t, :], ALU.mult, ALU.add)
            last.then_inc(s_ln2, 1)
            dv.wait_ge(s_ln2, 2)
            for t in range(NT):
                last = v.scalar_tensor_tensor(y2[:, t, :], y2[:, t, :], bd(w_2, t), y1[:, t, :], ALU.mult, ALU.add)
            last.then_inc(s_ln2, 1)
            dv.wait_ge(s_ln2, 3)
            for t in range(NT):
                last = v.bn_stats(bn[:, t, :], y2[:, t, :])
            last.then_inc(s_ln2, 1)
            dv.wait_ge(s_ln2, 4)
            for t in range(NT):
                last = v.bn_aggr(mv[:, t, :], bn[:, t, :])
            last.then_inc(s_ln2, 1)
            dv.wait_ge(s_ln2, 5)
            v.tensor_scalar(var[:], mv[:, :, 1], EPS, None, ALU.add).then_inc(s_ln4, 1)
            dv.wait_ge(s_pw, 4)
            for t in range(NT):
                last = v.tensor_scalar(y2[:, t, :], y2[:, t, :], mv[:, t, 0:1], rstd[:, t:t + 1],
                                       ALU.subtract, ALU.mult)
            last.then_inc(s_ln2, 1)
            dv.wait_ge(s_ln2, 6)
            v.tensor_tensor(res[:], y2[:], x1[:], ALU.add).then_inc(s_fin, 1)

        @block.tensor
        def _(pe):
            t_ = nc.tensor
            pe.wait_ge(s_const, 16)
            pe.wait_ge(s_p, 1)

            def scores(b):
                pe.wait_ge(s_xn, b + 1)
                if b >= 2:
                    pe.wait_ge(s_xtc, b - 1)
                for t in range(4):
                    last = t_.transpose(bank[b % 2][:, 128 * t:128 * t + 128], xn[:, 4 * b + t, :], ident)
                last.then_inc(s_xt, 1)
                pe.wait_ge(s_xtc, b + 1)
                if b >= 2:
                    pe.wait_ge(s_ex, 2 * (b - 1))
                for t in range(4):
                    xt = xnT[:, 4 * b + t, :]
                    last = t_.matmul(bank[2 + b % 2][:, 128 * t:128 * t + 128], xt, xt, start=True, stop=True)
                last.then_inc(s_sc, 1)

            def attend(b):
                pe.wait_ge(s_ex, 2 * (b + 1))
                if b >= 2:
                    pe.wait_ge(s_pvu, b - 1)
                for t in range(4):
                    p = P[:, 4 * b + t, :]
                    t_.matmul(bank[4 + b % 2][:, 128 * t:128 * t + 128], p, xn[:, 4 * b + t, :], start=True, stop=True)
                    last = t_.matmul(bank[6 + b % 2][:, 2 * t:2 * t + 2], p, ones[:], start=True, stop=True)
                last.then_inc(s_pv, 1)

            for b in range(B):
                scores(b)
                if b:
                    attend(b - 1)
            attend(B - 1)
            pe.wait_ge(s_w, 64)
            for b in range(B):
                pe.wait_ge(s_h, b + 1)
                if b >= 2:
                    pe.wait_ge(s_htc, b - 1)
                for t in range(4):
                    last = t_.transpose(bank[b % 2][:, 128 * t:128 * t + 128], h[:, 4 * b + t, 0:D], ident)
                last.then_inc(s_ht, 1)
            for b in range(B):
                pe.wait_ge(s_htc, b + 1)
                for t in range(4 * b, 4 * b + 4):
                    last = t_.matmul(bank[6][:, 256 + E * t:256 + E * t + E], hT[:, 128 * t:128 * t + 128], gw[:],
                                     start=True, stop=True)
            last.then_inc(s_lg, 1)
            pe.wait_ge(s_asg, 1)
            t_.matmul(bank[6][:, 0:256], onesb[:], asg[:, :, :].rearrange("p t e -> p (t e)"), start=True, stop=True).then_inc(s_nct, 1)
            pe.wait_ge(s_wm, 1)
            for rp in range(2):
                for c in range(CH):
                    last = t_.matmul(bank[7][:, 128 * rp:128 * rp + 128], wmP[:, 2 * c + rp, :], ident,
                                     start=c == 0, stop=c == CH - 1)
            last.then_inc(s_kt, 1)

            def up(c, k):
                pe.wait_ge(s_gu, 4 * c + k - 1 if k else less_one(4 * c, 16))
                sh, hb = k // HB, k % HB
                xt = hT[:, bass.ds(c * 512, 512)]
                t_.matmul(bank[k % 2][:], w1s[:, sh, 128 * hb:128 * hb + 128], xt, start=True, stop=True)
                t_.matmul(bank[2 + k % 2][:], w3s[:, sh, 128 * hb:128 * hb + 128], xt, start=True, stop=True).then_inc(s_up, 1)

            pe.wait_ge(s_list, 1)
            with pe.Fori(0, 4) as c:
                for k in range(S * HB):
                    up(c, k)
                    pe.wait_ge(s_cnt, c * 4 + k + 1)
                    t_.matmul(bank[6][:, 0:3], blockb[:], cnt[:], start=True, stop=True).then_inc(s_tot, 1)
                pe.wait_ge(s_gu, c * 4 + 4)
                pe.wait_ge(s_shc, c)
                for t in range(4):
                    for k in range(S * HB):
                        last = t_.matmul(bank[4][:, 128 * t:128 * t + 128], gu[:, k, 128 * t:128 * t + 128], w2s[:, k, :],
                                         start=k == 0, stop=k == S * HB - 1)
                last.then_inc(s_dn, 1)
            pe.wait_ge(s_eq, 1)
            block = cst[:, C_BLOCK:C_BLOCK + 128]
            t_.matmul(bank[6][:, 0:2], block, tot[:], start=True, stop=True)
            t_.matmul(bank[6][:, 2:4], beforef, tot[:], start=True, stop=True).then_inc(s_eqt, 1)
            pe.wait_ge(s_sl, 1)
            t_.matmul(bank[6][:, 0:2], beforef, tot[:], start=True, stop=True).then_inc(s_slt, 1)
            pe.wait_ge(s_R, 1)
            t_.matmul(bank[7][:, 0:CW + 1], deltah[:], R[:], start=True, stop=True).then_inc(s_D, 1)
            n = pe.value_load(elist_i[0:1, E:E + 1], min_val=2, max_val=E)
            pe.wait_ge(s_Dc, 1)
            with pe.Fori(0, E) as j:
                with pe.If(j < n):
                    pe.wait_ge(s_ge, j + 1)
                    pe.wait_ge(s_tok, j)
                    for m in range(3):
                        last = t_.matmul(bank[m][:, 0:CW + 1], ge[:, 0, 128 * m:128 * m + 128], Dl[:], start=True, stop=True)
                    last.then_inc(s_G, 1)
            with pe.Fori(0, E - 1, 2) as i:
                for k in range(2):
                    with pe.If(i + k < n):
                        j = i + k
                        pe.wait_ge(s_gat[k], 24 * i + 48)
                        pe.wait_ge(s_tok, n)
                        pe.wait_ge(s_gtc, j)
                        for m, rows in enumerate(SLOT_ROWS):
                            last = t_.transpose(bank[0][:, 128 * m:128 * m + rows], xg[0:rows, k, m, 0:D],
                                                ident[0:rows, 0:rows])
                        last.then_inc(s_gt, 1)
                        pe.wait_ge(s_wl[k], 24 * i + 48)
                        pe.wait_ge(s_gtc, j + 1)
                        pe.wait_ge(s_eg, 2 * j)
                        for hb in range(HB):
                            t_.matmul(bank[1 + hb][:, 0:CAP], w1e[:, k, 128 * hb:128 * hb + 128], xgT[:, k], start=True, stop=True)
                            t_.matmul(bank[3 + hb][:, 0:CAP], w3e[:, k, 128 * hb:128 * hb + 128], xgT[:, k],
                                      start=True, stop=True).then_inc(s_eu, 1)
                        pe.wait_ge(s_eg, 2 * j + 2)
                        pe.wait_ge(s_yc, j)
                        for m, rows in enumerate(SLOT_ROWS):
                            for hb in range(HB):
                                last = t_.matmul(bank[5][0:rows, 128 * m:128 * m + 128], gue[:, hb, 128 * m:128 * m + rows],
                                                 w2e[:, k, hb, :], start=hb == 0, stop=hb == HB - 1)
                        last.then_inc(s_ed, 1)


_INS = ["L0_attn_x", "L0_ffn_gate_w", "L0_ffn_gate_b", "L0_ffn_ew1", "L0_ffn_ew3", "L0_ffn_ew2",
        "L0_ffn_sw1", "L0_ffn_sw3", "L0_ffn_sw2"]


def kernel(**inputs):
    import numpy as _np
    import concourse.bacc as _bacc
    from concourse import mybir as _mybir
    from concourse.bass_utils import run_bass_kernel_spmd as _run

    nc = _bacc.Bacc("TRN2", target_bir_lowering=False, num_devices=1)
    arrays, args = {}, []
    for name in _INS:
        a = _np.ascontiguousarray(inputs[name])
        if name == "L0_attn_x":
            a = a.reshape(N, D)
        arrays[f"in_{name}"] = a
        args.append(nc.dram_tensor(f"in_{name}", a.shape, _mybir.dt.from_np(a.dtype), kind="ExternalInput").ap())
    arrays["in_constants"] = constants()
    args.append(nc.dram_tensor("in_constants", (128, C_ALL), _mybir.dt.float32, kind="ExternalInput").ap())
    args.append(nc.dram_tensor("out_0", (N, D), _mybir.dt.float32, kind="ExternalOutput").ap())
    build(nc, *args)
    r = _run(nc, [arrays], core_ids=[0])
    return r.results[0]["out_0"].reshape(B, T, D)
```

```python
from contextlib import ExitStack

import concourse.bass as bass
import numpy as np
from concourse import mybir

B, T, D, E, H, S = 4, 512, 128, 16, 256, 2
N = B * T
NT = N // 128
CAP = 320
CH = 8
CW = N // CH
HB = H // 128
SLOT_ROWS = (128, 128, 64)
HW = 132
EPS = 1e-5
UNASSIGNED = -3.0e38
ROUNDS = 8
SU = S * HB
ZEROED = 32
START = 2

C_ID, C_BLOCK, C_BEFORE, C_DELTA = 0, 128, 256, 384
C_IOTA = 512
C_CAND = C_IOTA + 384
C_STEP = C_CAND + 3 * ROUNDS
C_REV = C_STEP + ROUNDS
C_EIX = C_REV + E
C_SLOT = C_EIX + E
C_GBASE = C_SLOT + 3
C_CBASE = C_GBASE + 1
C_JIX = C_CBASE + 1
C_PAD = C_JIX + E * E
C_ALL = C_PAD + HW


def constants():
    c = np.zeros((128, C_ALL), np.float32)
    p = np.arange(128)
    c[:, C_ID:C_ID + 128] = np.eye(128)
    same = p[:, None] // CH == p[None, :] // CH
    c[:, C_BLOCK:C_BLOCK + 128] = same
    c[:, C_BEFORE:C_BEFORE + 128] = same & (p[:, None] < p[None, :])
    c[:, C_DELTA:C_DELTA + 128] = np.eye(128) - np.eye(128, k=1)
    c[:, C_IOTA:C_IOTA + 384] = np.arange(384)
    for k in range(ROUNDS):
        step = 4 ** (ROUNDS - 1 - k)
        c[:, C_CAND + 3 * k:C_CAND + 3 * k + 3] = step * np.arange(1, 4)
        c[:, C_STEP + k] = step
    c[:, C_REV:C_REV + E] = E - np.arange(E)
    c[:, C_EIX:C_EIX + E] = np.arange(E)
    for k in range(3):
        c[:, C_SLOT + k] = p + 128 * k
    c[:, C_GBASE] = CAP * (p // CH)
    c[:, C_CBASE] = CW * (p % CH)
    c[:, C_JIX:C_JIX + E * E] = np.repeat(np.arange(E), E)
    c[:, C_PAD + D] = -1.0
    return c


def build(nc, x, gate_w, gate_b, ew1, ew3, ew2, sw1, sw3, sw2, consts, out):
    f32, bf16, f16, i32 = mybir.dt.float32, mybir.dt.bfloat16, mybir.dt.float16, mybir.dt.int32
    ALU, ACT, AX = mybir.AluOpType, mybir.ActivationFunctionType, mybir.AxisListType.X
    v, s_, g_ = nc.vector, nc.scalar, nc.gpsimd

    ctx = ExitStack()
    with ctx:
        def sb(name, shape, dt=f32):
            return ctx.enter_context(nc.sbuf_tensor(name, shape, dt))

        def sem(name):
            return ctx.enter_context(nc.semaphore(name))

        htab = nc.dram_tensor("htab", [N + 1, HW], f32).ap()
        ytab = nc.dram_tensor("ytab", [2 * N, D], f32).ap()

        def tiled(ap):
            v = ap.rearrange("(a q rp r2) d -> r2 rp q a d", q=64, rp=2, r2=2)
            return [[v[r2][rp] for rp in range(2)] for r2 in range(2)]

        def tiles(buf):
            v = buf[:, :, :].rearrange("p (a rp) d -> p rp a d", rp=2)
            return [[v[64 * r2:64 * r2 + 64, rp] for rp in range(2)] for r2 in range(2)]

        def move(eng, dst, src, done):
            for r2 in range(2):
                for rp in range(2):
                    eng.dma_start(dst[r2][rp], src[r2][rp]).then_inc(done, 16)

        def less_one(i, top):
            return (i * (top - 1)) >> (top.bit_length() - 1)

        cst = sb("cst", [128, C_ALL])
        xs_in = sb("x_in", [128, NT, D])
        xn = sb("xn", [128, NT, D + 2])
        xnT = sb("xnT", [128, NT, 128])
        P = sb("P", [128, NT, 128])
        x1 = sb("x1", [128, NT, D])
        h = sb("h", [128, NT, HW])
        hT = sb("hT", [128, NT * 128])
        ones = sb("ones", [128, 2])
        zeros = sb("zeros", [128, 1024])
        bn = [sb(f"bn{k}", [128, NT, 6]) for k in range(4)]
        mv = [sb(f"mv{k}", [128, NT, 2]) for k in range(4)]
        var = [sb(f"var{k}", [128, NT]) for k in range(4)]
        rstd = [sb(f"rstd{k}", [128, NT]) for k in range(4)]
        nmean = [sb(f"nmean{k}", [128, NT]) for k in range(4)]
        shift = [sb(f"shift{k}", [128, NT]) for k in range(4)]
        lsum = sb("lsum", [128, NT])
        lsq = sb("lsq", [128, NT])
        half = sb("half", [128, 4])
        lg = sb("lg", [128, NT, E])
        mx = sb("mx", [128, NT])
        ex = sb("ex", [128, NT, E])
        sc = sb("sc", [128, NT, E])
        tA = sb("tA", [128, NT, E])
        oh1 = sb("oh1", [128, NT, E])
        oh2 = sb("oh2", [128, NT, E])
        asg = sb("asg", [128, NT, E], bf16)
        first = sb("first", [128, NT])
        second = sb("second", [128, NT])
        w_1 = sb("w_1", [128, NT])
        w_2 = sb("w_2", [128, NT])
        bias = sb("bias", [128, E])
        gw = sb("gw", [128, E])
        wmP = sb("wmP", [128, 2, E, CH])
        onesb = sb("onesb", [128, 128], bf16)
        blockb = sb("blockb", [128, 128], bf16)
        beforef = cst[:, C_BEFORE:C_BEFORE + 128]
        deltah = sb("deltah", [128, 128], f16)
        ident = cst[:, C_ID:C_ID + 128]
        act = sb("act", [128, E])
        rank = sb("rank", [128, E])
        hit = sb("hit", [128, E, E])
        elist = sb("elist", [128, E])
        e320 = sb("e320", [128, E + 1])
        elist_i = sb("elist_i", [128, E + 1], i32)
        K = sb("K", [128, CW])
        m32 = sb("m32", [128, CW], i32)
        u32 = sb("u32", [128, CW], i32)
        part = sb("part", [128, CW], i32)
        hi = sb("hi", [128, CW])
        lo = sb("lo", [128, CW])
        key2 = sb("key2", [128, CW])
        assigned = sb("assigned", [128, CW])
        junk = sb("junk", [128, 3, CW])
        above = sb("above", [128, CW])
        base = sb("base", [128, 1])
        hbase = sb("hbase", [128, 1])
        cand = sb("cand", [128, 3])
        nextc = sb("nextc", [128, 3])
        cnt = sb("cnt", [128, 3], bf16)
        dec3 = sb("dec3", [128, 3])
        dec = sb("dec", [128, 1])
        tot = sb("tot", [128, 2])
        eqm = sb("eqm", [128, CW])
        eqs = sb("eqs", [128, CW])
        sel = sb("sel", [128, CW])
        selp = sb("selp", [128, CW])
        rem = sb("rem", [128, 1])
        off = sb("off", [128, 1])
        gstart = sb("gstart", [128, 1])
        R = sb("R", [128, CW + 1], f16)
        Dl = sb("Dl", [128, CW + 1], f16)
        w1s = sb("w1s", [128, S, H])
        w3s = sb("w3s", [128, S, H])
        w2s = sb("w2s", [128, S * HB, D])
        sil = sb("sil", [128, 2, 512])
        gu = sb("gu", [128, 4 * SU, 512])
        shared = sb("shared", [128, NT, D])
        ge = sb("ge", [128, 2, 384], f16)
        tokf = sb("tokf", [128, E * 3 + 3])
        idx = sb("idx", [128, 2, 3], i32)
        ne1 = sb("ne1", [128, 2, 3])
        dst = sb("dst", [128, 2, 3], i32)
        wdiff = sb("wdiff", [128, 2, 3])
        wslot = sb("wslot", [128, 2, 3])
        xg = sb("xg", [128, 2, 3, HW])
        xgT = sb("xgT", [128, 2, CAP])
        w1e = sb("w1e", [128, 2, H])
        w3e = sb("w3e", [128, 2, H])
        w2e = sb("w2e", [128, 2, HB, D])
        sile = sb("sile", [128, HB, CAP])
        gue = sb("gue", [128, HB, CAP])
        ye = sb("ye", [128, 2, 3, D])
        y = sb("y", [128, 2 * NT, D])
        total = sb("total", [128, NT, D])
        res = xs_in

        bank = [ctx.enter_context(nc.psum_tensor(f"bank{i}", [128, 512], f32)) for i in range(8)]

        P_BANK = ((0, 1, 2), (3, 5, 6))
        G_BANK, U_BANK = (1, 2), (3, 5)

        def down_bank(c):
            return bank[(4, 7)[c % 2]]

        def attended_pair(t):
            return bank[4 + (t // 2) % 4][:, 0:2 * (D + 2)].rearrange("p (t d) -> p t d", t=2)

        def attended(t):
            return attended_pair(t)[:, t % 2, :]

        def of_slot(ap, j):
            return ap[:, bass.ds(j, 1)]

        def load_tiles(eng, buf, src, half_, done):
            a = CH // 2 * half_
            for r2 in range(2):
                for rp in range(2):
                    eng.dma_start(tiles(buf)[r2][rp][:, a:a + CH // 2], tiled(src)[r2][rp][:, a:a + CH // 2]).then_inc(done, 16)
        s_const, s_w, s_bias = sem("const_loaded"), sem("weights_loaded"), sem("bias_loaded")
        s_x = [sem("x_first_half_loaded"), sem("x_second_half_loaded")]
        s_zero, s_pad, s_hw = sem("zeros_set"), sem("pad_row_written"), sem("htab_written")
        s_half, s_set, s_cc = sem("half_set"), sem("fills_set"), sem("constants_cast")
        s_var = [sem(f"var{k}_ready") for k in range(4)]
        s_r = [sem(f"rstd{k}_ready") for k in range(4)]
        s_xn, s_xt, s_xtc = sem("xn_ready"), sem("x_transposed"), sem("xT_copied")
        s_sc, s_ex, s_pv, s_a2 = sem("scores_ready"), sem("probs_ready"), sem("attn_ready"), sem("attn_normed")
        s_h, s_ht, s_htc, s_lg = sem("h_ready"), sem("h_transposed"), sem("hT_copied"), sem("logits_ready")
        s_lmx, s_gex = sem("logits_centred"), sem("gate_exp_ready")
        s_h1 = sem("choices_in_h")
        s_asg, s_nct = sem("assigned_ready"), sem("expert_counts_ready")
        s_list = sem("list_ready")
        s_wm, s_kt = sem("masked_logits_ready"), sem("expert_major_ready")
        s_cnt, s_tot = sem("counts_ready"), sem("totals_ready")
        s_up, s_sil, s_gu, s_dn, s_shc = (sem("shared_up_done"), sem("shared_silu_done"), sem("shared_gu_done"),
                                          sem("shared_down_done"), sem("shared_copied"))
        s_eq, s_eqt, s_sl, s_slt, s_R, s_D, s_Dc = (sem("ties_counted"), sem("tie_totals"), sem("selected_counted"),
                                              sem("selected_totals"), sem("rows_ready"), sem("differences_ready"),
                                              sem("differences_copied"))
        s_ge, s_G, s_tok = sem("slots_compared"), sem("prefix_rows_ready"), sem("tokens_of_slots")
        s_wl = [sem("expert_weights_even"), sem("expert_weights_odd")]
        s_gat = [sem("rows_gathered_even"), sem("rows_gathered_odd")]
        s_sct = [sem("rows_scattered_even"), sem("rows_scattered_odd")]
        s_idx, s_dst = sem("index_copied"), sem("destinations_ready")
        s_gt, s_gtc = sem("gathered_transposed"), sem("gathered_T_copied")
        s_eu, s_es, s_eg, s_ed, s_yc = (sem("expert_up_done"), sem("expert_silu_done"), sem("expert_gu_done"),
                                        sem("expert_down_done"), sem("expert_out_copied"))
        s_yl = [sem("y_first_half_loaded"), sem("y_second_half_loaded")]
        s_n4, s_fin, s_out = sem("result_normed"), sem("result_ready"), sem("out_written")
        s_v, s_dv = sem("vector_step"), sem("vector_end_step")
        counts_from_start = (s_gu, s_gt, s_dst, s_yc, s_gtc, s_eg, s_ed, s_tok, s_G)

        def places(eng, n, body):
            with eng.Fori(0, E - 1, 2) as i:
                for k in range(2):
                    with eng.If(i + k < n):
                        body(i + k, k)

        def in_use(eng):
            return eng.value_load(elist_i[0:1, E:E + 1], min_val=2, max_val=E)

        block = ctx.enter_context(nc.Block())

        @block.sync
        def _(sp):
            for s in counts_from_start:
                sp.sem_inc(s, START)
            load_tiles(sp, xs_in, x, 0, s_x[0])
            load_tiles(sp, xs_in, x, 1, s_x[1])
            sp.dma_start(gw[:], gate_w).then_inc(s_w, 16)
            sp.dma_start(w1s[:], sw1.rearrange("s d h -> d s h")).then_inc(s_w, 16)
            sp.dma_start(w3s[:], sw3.rearrange("s d h -> d s h")).then_inc(s_w, 16)
            sp.dma_start(w2s[:], sw2.rearrange("s (k p) d -> p (s k) d", p=128)).then_inc(s_w, 16)
            sp.dma_start(bias[:], gate_b.rearrange("(o e) -> o e", o=1).broadcast_to([128, E])).then_inc(s_bias, 16)
            sp.wait_ge(s_const, 16)
            sp.dma_start(htab[N:N + 1, :], cst[0:1, C_PAD:C_PAD + HW]).then_inc(s_pad, 16)
            sp.wait_ge(s_h1, 1)
            move(sp, tiled(htab[0:N, :]), tiles(h), s_hw)
            sp.wait_ge(s_list, 1)
            n = in_use(sp)

            def load_weights(j, k):
                e = sp.value_load(elist_i[0:1, bass.ds(j, 1)], min_val=0, max_val=E - 1)
                sp.wait_ge(s_ed, j - 1 + START)
                sp.dma_start(w1e[:, k], ew1[bass.ds(e, 1)].rearrange("o d h -> d (o h)")).then_inc(s_wl[k], 16)
                sp.dma_start(w3e[:, k], ew3[bass.ds(e, 1)].rearrange("o d h -> d (o h)")).then_inc(s_wl[k], 16)
                sp.dma_start(w2e[:, k], ew2[bass.ds(e, 1)].rearrange("o (k p) d -> p (o k) d", p=128)).then_inc(s_wl[k], 16)

            places(sp, n, load_weights)
            sp.wait_ge(s_sct[0], 48 * ((n + 1) // 2) + ZEROED)
            sp.wait_ge(s_sct[1], 48 * (n // 2) + ZEROED)
            for half_ in range(2):
                src, dst_ = tiled(ytab[:, :]), tiles(y)
                a = CH // 2 * half_
                for c in range(2):
                    for r2 in range(2):
                        for rp in range(2):
                            sp.dma_start(dst_[r2][rp][:, CH * c + a:CH * c + a + CH // 2],
                                         src[r2][rp][:, CH * c + a:CH * c + a + CH // 2]).then_inc(s_yl[half_], 16)
            for half_ in range(2):
                sp.wait_ge(s_fin, 2 * half_ + 2)
                a = CH // 2 * half_
                for r2 in range(2):
                    for rp in range(2):
                        sp.dma_start(tiled(out)[r2][rp][:, a:a + CH // 2],
                                     tiles(res)[r2][rp][:, a:a + CH // 2]).then_inc(s_out, 16)
            sp.wait_ge(s_out, 128)

        @block.gpsimd
        def _(pool):
            pool.memset(half[:], -0.5).then_inc(s_half, 1)
            pool.memset(zeros[:], 0.0).then_inc(s_zero, 1)
            pool.wait_ge(s_zero, 1)
            for k in range(4):
                pool.dma_start(ytab[N // 2 * k:N // 2 * (k + 1), :].rearrange("(p r) d -> p (r d)", p=128),
                               zeros[:, :]).then_inc(s_sct[k // 2], 16)
            pool.wait_ge(s_half, 1)

            def normalise(k, b, shifted):
                q = slice(4 * b, 4 * b + 4)
                pool.wait_ge(s_var[k], b + 1)
                g_.tensor_tensor(rstd[k][:, q], var[k][:, q], half[:], ALU.pow).then_inc(s_r[k], 1)
                if shifted:
                    pool.wait_ge(s_r[k], 2 * b + 1)
                    g_.tensor_tensor(shift[k][:, q], nmean[k][:, q], rstd[k][:, q], ALU.mult).then_inc(s_r[k], 1)

            for b in range(B):
                normalise(0, b, True)
                if b == 0:
                    g_.memset(xn[:, :, D:D + 2], 1.0)
                    g_.memset(P[:], 0.0).then_inc(s_set, 1)
            for b in range(B + 1):
                if b < B:
                    normalise(1, b, True)
                if b == 0:
                    pool.wait_ge(s_const, 16)
                    g_.tensor_copy(blockb[:], cst[:, C_BLOCK:C_BLOCK + 128])
                    g_.tensor_copy(deltah[:], cst[:, C_DELTA:C_DELTA + 128]).then_inc(s_cc, 1)
                    g_.memset(onesb[:], 1.0)
                    g_.memset(ones[:], 1.0)
                    g_.memset(xg[:], 0.0).then_inc(s_set, 1)
                if b:
                    normalise(2, b - 1, False)
            pool.wait_ge(s_sct[1], ZEROED)
            pool.wait_ge(s_pad, 16)
            pool.wait_ge(s_list, 1)
            n = in_use(pool)
            last_token, last_result = pool.to_reg(N), pool.to_reg(2 * N - 1)

            def gather(j, k):
                pool.wait_ge(s_gt, j - 1 + START)
                pool.wait_ge(s_dst, j - 1 + START)
                pool.wait_ge(s_tok, j + 1 + START)
                g_.tensor_copy(idx[:, k], tokf[:, bass.ds(3 * j, 3)]).then_inc(s_idx, 1)
                pool.wait_ge(s_hw, 64)
                pool.wait_ge(s_idx, j + 1)
                for m, rows in enumerate(SLOT_ROWS):
                    g_.indirect_dma_start(
                        out=xg[0:rows, k, m, :], out_offset=None, in_=htab[:, :],
                        in_offset=bass.IndirectOffsetOnAxis(ap=idx[0:rows, k, m:m + 1], axis=0),
                        bounds_check=last_token, oob_is_err=False).then_inc(s_gat[k], 16)

            def scatter(j, k):
                this = pool.compute_val(j + 1 + START)
                pool.wait_ge(s_sct[0], ZEROED)
                pool.wait_ge(s_dst, this)
                pool.wait_ge(s_yc, this)
                for m, rows in enumerate(SLOT_ROWS):
                    g_.indirect_dma_start(
                        out=ytab[:, :], out_offset=bass.IndirectOffsetOnAxis(ap=dst[0:rows, k, m:m + 1], axis=0),
                        in_=ye[0:rows, k, m, :], in_offset=None,
                        bounds_check=last_result, oob_is_err=False).then_inc(s_sct[k], 16)

            gather(0, 0)
            with pool.Fori(0, E - 1, 2) as i:
                for k in range(2):
                    with pool.If(i + k + 1 < n):
                        gather(i + k + 1, 1 - k)
                    with pool.If(i + k < n):
                        scatter(i + k, k)
            for b in range(B):
                normalise(3, b, True)
                if b:
                    pool.wait_ge(s_n4, b)
                    g_.tensor_tensor(res[:, 4 * b - 4:4 * b, :], total[:, 4 * b - 4:4 * b, :],
                                     x1[:, 4 * b - 4:4 * b, :], ALU.add).then_inc(s_fin, 1)

        @block.scalar
        def _(ac):
            ac.dma_start(cst[:], consts).then_inc(s_const, 16)

            def norm(k, t, dst_, src):
                return s_.activation(dst_, src, ACT.Identity, bias=shift[k][:, t:t + 1], scale=rstd[k][:, t:t + 1])

            def norm_x(b):
                ac.wait_ge(s_r[0], 2 * b + 2)
                for t in range(4 * b, 4 * b + 4):
                    last = norm(0, t, xn[:, t, 0:D], xs_in[:, t, :])
                last.then_inc(s_xn, 1)

            def copy_xT(b):
                ac.wait_ge(s_xt, b + 1)
                s_.activation(xnT[:, 4 * b:4 * b + 4, :], bank[b % 2][:, :], ACT.Identity).then_inc(s_xtc, 1)

            def exponentials(b):
                ac.wait_ge(s_sc, b + 1)
                ac.wait_ge(s_set, 1)
                sc4 = bank[2 + b % 2][:, :].rearrange("p (t k) -> p t k", t=4)
                for r2 in range(2):
                    q = slice(64 * r2, 64 * r2 + 64)
                    s_.activation(P[q, 4 * b:4 * b + 4, q], sc4[q, :, q], ACT.Exp, scale=float(D) ** -0.5).then_inc(s_ex, 1)

            def norm_attention(b):
                ac.wait_ge(s_r[1], 2 * b + 2)
                for t in range(4 * b, 4 * b + 4):
                    last = norm(1, t, x1[:, t, :], attended(t)[:, 0:D])
                last.then_inc(s_a2, 1)

            def copy_hT(b):
                ac.wait_ge(s_ht, b + 1)
                s_.activation(hT[:, 512 * b:512 * b + 512], bank[b % 2][:, :], ACT.Identity).then_inc(s_htc, 1)

            norm_x(0), norm_x(1)
            copy_xT(0), norm_x(2), copy_xT(1), norm_x(3), exponentials(0)
            copy_xT(2), exponentials(1), norm_attention(0)
            copy_xT(3), exponentials(2), norm_attention(1)
            exponentials(3), copy_hT(0), norm_attention(2), copy_hT(1), norm_attention(3), copy_hT(2), copy_hT(3)
            ac.wait_ge(s_lmx, 1)
            s_.activation(ex[:], sc[:], ACT.Exp).then_inc(s_gex, 1)
            s_.preload_act_table(ACT.Silu)
            with ac.Fori(0, 4) as c:
                for k in range(SU):
                    ac.wait_ge(s_up, c * SU + k + 1)
                    ac.wait_ge(s_gu, c * SU + k - 1 + START)
                    s_.activation(sil[:, k % 2], bank[k % 2][:], ACT.Silu).then_inc(s_sil, 1)

            def copy_shared(c):
                ac.wait_ge(s_dn, c + 1)
                s_.activation(shared[:, 4 * c:4 * c + 4, :], down_bank(c)[:], ACT.Identity).then_inc(s_shc, 1)

            copy_shared(0)
            n = in_use(ac)

            def expert(j, k):
                ac.wait_ge(s_gt, j + 1 + START)
                s_.activation(xgT[:, k], bank[0][:, 0:CAP], ACT.Identity).then_inc(s_gtc, 1)
                for hb in range(HB):
                    ac.wait_ge(s_eu, 2 * j + hb + 1)
                    s_.activation(sile[:, hb], bank[G_BANK[hb]][:, 0:CAP], ACT.Silu).then_inc(s_es, 1)
                ac.wait_ge(s_ed, j + 1 + START)
                ac.wait_ge(s_sct[k], 24 * (j - k) + ZEROED)
                ac.wait_ge(s_dst, j + 1 + START)
                for m, rows in enumerate(SLOT_ROWS):
                    last = s_.activation(ye[0:rows, k, m], bank[6][0:rows, 128 * m:128 * m + 128], ACT.Identity,
                                         scale=wslot[0:rows, k, m:m + 1])
                last.then_inc(s_yc, 1)

            places(ac, n, expert)
            for c in range(1, 4):
                copy_shared(c)
            for b in range(B):
                ac.wait_ge(s_r[3], 2 * b + 2)
                for t in range(4 * b, 4 * b + 4):
                    last = norm(3, t, total[:, t, :], total[:, t, :])
                last.then_inc(s_n4, 1)

        @block.vector
        def _(dv):
            done = [0]

            def link(ins):
                done[0] += 1
                ins.then_inc(s_v, 1)
                dv.wait_ge(s_v, done[0])

            def negate_mean(k, b):
                q = slice(4 * b, 4 * b + 4)
                v.tensor_scalar(nmean[k][:, q], mv[k][:, q, 0], -1.0, None, ALU.mult)

            def stats(k, b, src):
                for t in range(4 * b, 4 * b + 4):
                    last = v.bn_stats(bn[k][:, t, :], src(t))
                link(last)
                for t in range(4 * b, 4 * b + 4):
                    last = v.bn_aggr(mv[k][:, t, :], bn[k][:, t, :])
                link(last)
                if k < 2:
                    negate_mean(k, b)

            def variance(k, b):
                q = slice(4 * b, 4 * b + 4)
                v.tensor_scalar(var[k][:, q], mv[k][:, q, 1], EPS, None, ALU.add).then_inc(s_var[k], 1)

            def bc(ap):
                return ap[:, :].rearrange("p (t o) -> p t o", o=1).broadcast_to([128, NT, E])

            for b in range(B):
                dv.wait_ge(s_x[b // 2], 64)
                stats(0, b, lambda t: xs_in[:, t, :])
                variance(0, b)
            for b in range(B + 1):
                if b < B:
                    q = slice(4 * b, 4 * b + 4)
                    dv.wait_ge(s_pv, b + 1)
                    for t in (4 * b, 4 * b + 2):
                        v.tensor_copy(lsum[:, t:t + 2], attended_pair(t)[:, :, D])
                    stats(1, b, lambda t: attended(t)[:, 0:D])
                    link(v.scalar_tensor_tensor(lsq[:, q], lsum[:, q], EPS * 16, lsum[:, q], ALU.mult, ALU.mult))
                    v.tensor_tensor(var[1][:, q], lsq[:, q], mv[1][:, q, 1], ALU.add).then_inc(s_var[1], 1)
                if b:
                    q = slice(4 * b - 4, 4 * b)
                    dv.wait_ge(s_a2, b)
                    link(v.tensor_tensor(x1[:, q, :], x1[:, q, :], xs_in[:, q, :], ALU.add))
                    stats(2, b - 1, lambda t: x1[:, t, :])
                    variance(2, b - 1)
                    dv.wait_ge(s_r[2], b)
                    for t in range(4 * b - 4, 4 * b):
                        last = v.tensor_scalar(h[:, t, 0:D], x1[:, t, :], mv[2][:, t, 0:1], rstd[2][:, t:t + 1],
                                               ALU.subtract, ALU.mult)
                    last.then_inc(s_h, 1)
            dv.wait_ge(s_lg, 1)
            link(v.tensor_copy(lg[:], bank[2][:, 0:256]))
            link(v.tensor_reduce(mx[:], lg[:], AX, ALU.max))
            v.tensor_tensor(sc[:], lg[:], bc(mx), ALU.subtract).then_inc(s_lmx, 1)
            dv.wait_ge(s_gex, 1)
            link(v.tensor_reduce(mx[:], ex[:], AX, ALU.add))
            link(v.reciprocal(first[:], mx[:]))
            link(v.tensor_tensor(sc[:], ex[:], bc(first), ALU.mult))
            dv.wait_ge(s_bias, 16)
            link(v.tensor_tensor(sc[:], sc[:], bias[:, :].rearrange("p (o e) -> p o e", o=1).broadcast_to([128, NT, E]), ALU.add))
            rev = cst[:, C_REV:C_REV + E].rearrange("p (o e) -> p o e", o=1).broadcast_to([128, NT, E])
            dv.wait_ge(s_const, 16)

            def best(oh, pick):
                link(v.tensor_reduce(mx[:], sc[:], AX, ALU.max))
                link(v.tensor_tensor(tA[:], sc[:], bc(mx), ALU.is_equal))
                link(v.tensor_tensor(tA[:], tA[:], rev, ALU.mult))
                link(v.tensor_reduce(pick[:], tA[:], AX, ALU.max))
                link(v.tensor_tensor(oh[:], rev, bc(pick), ALU.is_equal))

            best(oh1, first)
            link(v.scalar_tensor_tensor(sc[:], oh1[:], -1.0e30, sc[:], ALU.mult, ALU.add))
            best(oh2, second)
            link(v.tensor_tensor(asg[:], oh1[:], oh2[:], ALU.add))
            v.tensor_tensor(ex[:], asg[:], lg[:], ALU.mult)
            link(v.tensor_scalar(tA[:], asg[:], -1.0, -UNASSIGNED, ALU.add, ALU.mult))
            by_parity = "p (c rp) e -> p c rp e"
            v.tensor_tensor(wmP[:, :, :, :].rearrange("p rp e c -> p c rp e"), tA[:, :, :].rearrange(by_parity, rp=2),
                            ex[:, :, :].rearrange(by_parity, rp=2), ALU.add).then_inc(s_wm, 1)
            v.tensor_tensor(oh1[:], oh1[:], lg[:], ALU.mult)
            link(v.tensor_tensor(oh2[:], oh2[:], lg[:], ALU.mult))
            v.tensor_reduce(h[:, :, D + 1], oh1[:], AX, ALU.add)
            v.tensor_reduce(h[:, :, D + 2], oh2[:], AX, ALU.add)
            v.memset(h[:, :, D + 3], 0.0)
            v.tensor_scalar(h[:, :, D], first[:], -1.0, float(E), ALU.mult, ALU.add).then_inc(s_h1, 1)
            dv.wait_ge(s_kt, 1)
            link(v.tensor_scalar(K[:, :].rearrange("p (q rp r2) -> p rp r2 q", rp=2, r2=2),
                                 bank[7][:, 0:CW].rearrange("p (rp r2 q) -> p rp r2 q", rp=2, r2=2), 0.0, None, ALU.add))
            v.memset(base[:], 0.0)
            v.tensor_copy(cand[:], cst[:, C_CAND:C_CAND + 3])
            link(v.tensor_scalar(m32[:], K[:, :].bitcast(i32), 31, -2147483648, ALU.arith_shift_right, ALU.bitwise_or))
            link(v.tensor_tensor(u32[:], K[:, :].bitcast(i32), m32[:], ALU.bitwise_xor))
            link(v.tensor_scalar(part[:], u32[:], 16, None, ALU.logical_shift_right))
            link(v.tensor_copy(hi[:], part[:]))

            start = done[0]
            per_round, between = 4, 13

            def search(half_, key, c, i, k):
                nth = i * 4 + k
                steps = start + (half_ * ROUNDS + nth) * per_round + half_ * between
                for m in range(3):
                    last = v.tensor_scalar(junk[:, m], key[:], cand[:, m:m + 1], None, ALU.is_ge, ALU.add,
                                           accum_out=cnt[:, m:m + 1])
                last.then_inc(s_cnt, 1)
                v.tensor_scalar(nextc[:], cst[:, bass.ds(C_CAND + 3 * nth + 3, 3)], base[:, 0:1], None,
                                ALU.add).then_inc(s_v, 1)
                dv.wait_ge(s_sil, c * SU + k + 1)
                v.scalar_tensor_tensor(gu[:, bass.ds(c * SU + k, 1), :].rearrange("p o n -> p (o n)"), sil[:, k % 2], 1.0 / S, bank[2 + k % 2][:],
                                       ALU.mult, ALU.mult).then_inc(s_gu, 1)
                dv.wait_ge(s_tot, half_ * ROUNDS + nth + 1)
                v.tensor_scalar(dec3[:], bank[6][:, 0:3], float(CAP), None, ALU.is_ge, ALU.add,
                                accum_out=dec[:, 0:1]).then_inc(s_v, 1)
                dv.wait_ge(s_v, steps + 2)
                v.scalar_tensor_tensor(cand[:], dec[:, 0:1].broadcast_to([128, 3]), cst[:, bass.ds(C_STEP + nth, 1)],
                                       nextc[:], ALU.mult, ALU.add).then_inc(s_v, 1)
                v.scalar_tensor_tensor(base[:], dec[:], cst[:, bass.ds(C_STEP + nth, 1)], base[:],
                                       ALU.mult, ALU.add).then_inc(s_v, 1)
                dv.wait_ge(s_v, steps + 4)

            with dv.Fori(0, 2) as i:
                for k in range(4):
                    search(0, hi, i, i, k)
            done[0] += ROUNDS * per_round
            link(v.tensor_copy(hbase[:], base[:]))
            v.memset(base[:], 1.0)
            link(v.tensor_scalar(cand[:], cst[:, C_CAND:C_CAND + 3], 1.0, None, ALU.add))
            link(v.tensor_scalar(part[:], u32[:], 65535, None, ALU.bitwise_and))
            link(v.tensor_scalar(lo[:], part[:], 1.0, None, ALU.add))
            v.tensor_scalar(above[:], hi[:], hbase[:, 0:1], 65537.0, ALU.is_gt, ALU.mult)
            link(v.scalar_tensor_tensor(key2[:], hi[:], hbase[:, 0:1], lo[:], ALU.is_equal, ALU.mult))
            link(v.tensor_tensor(key2[:], key2[:], above[:], ALU.add))
            dv.wait_ge(s_nct, 1)
            link(v.tensor_reduce(act[:], bank[5][:, 0:256].rearrange("p (t e) -> p e t", e=E), AX, ALU.add))
            link(v.tensor_scalar(act[:], act[:], 1.0, None, ALU.min))
            link(v.tensor_tensor_scan(rank[:], ones[:, 0:1].broadcast_to([128, E]), act[:], 0.0, ALU.mult, ALU.add))
            v.tensor_scalar(mx[:], rank[:], -1.0, None, ALU.add)
            link(v.tensor_tensor(act[:], act[:], cst[:, C_EIX:C_EIX + E], ALU.mult))
            link(v.tensor_tensor(hit[:], cst[:, C_JIX:C_JIX + E * E].rearrange("p (j e) -> p j e", e=E),
                                 mx[:, :].rearrange("p (o e) -> p o e", o=1).broadcast_to([128, E, E]), ALU.is_equal))
            link(v.tensor_tensor(hit[:], hit[:], act[:, :].rearrange("p (o e) -> p o e", o=1).broadcast_to([128, E, E]), ALU.mult))
            link(v.tensor_reduce(elist[:], hit[:], AX, ALU.add))
            v.tensor_scalar(e320[:, 0:E], elist[:], float(CAP), None, ALU.mult)
            v.tensor_scalar(assigned[:], K[:], UNASSIGNED / 2, None, ALU.is_gt)
            v.tensor_copy(R[:, CW:CW + 1], cst[:, C_CBASE:C_CBASE + 1])
            v.tensor_copy(elist_i[:, E:E + 1], rank[:, E - 1:E])
            v.tensor_copy(elist_i[:, 0:E], elist[:]).then_inc(s_list, 1)
            assert done[0] == start + ROUNDS * per_round + between, done[0] - start - ROUNDS * per_round
            with dv.Fori(0, 2) as i:
                for k in range(4):
                    search(1, key2, i + 2, i, k)
            done[0] += ROUNDS * per_round
            v.tensor_scalar(above[:], key2[:], base[:, 0:1], None, ALU.is_gt, ALU.add, accum_out=tot[:, 0:1])
            link(v.scalar_tensor_tensor(eqm[:], key2[:], base[:, 0:1], assigned[:], ALU.is_equal, ALU.mult))
            one = ones[:, 0:1].broadcast_to([128, CW])
            link(v.tensor_tensor_scan(eqs[:], one, eqm[:], 0.0, ALU.mult, ALU.add))
            v.tensor_copy(tot[:, 1:2], eqs[:, CW - 1:CW]).then_inc(s_eq, 1)
            dv.wait_ge(s_eqt, 1)
            link(v.tensor_scalar(rem[:], bank[6][:, 0:1], -1.0, float(CAP), ALU.mult, ALU.add))
            link(v.tensor_tensor(rem[:], rem[:], bank[6][:, 3:4], ALU.subtract))
            link(v.scalar_tensor_tensor(eqs[:], eqs[:], rem[:, 0:1], eqm[:], ALU.is_le, ALU.mult))
            link(v.tensor_tensor(sel[:], eqs[:], above[:], ALU.add))
            link(v.tensor_tensor_scan(selp[:], one, sel[:], 0.0, ALU.mult, ALU.add))
            v.tensor_copy(tot[:, 0:1], selp[:, CW - 1:CW]).then_inc(s_sl, 1)
            dv.wait_ge(s_slt, 1)
            link(v.tensor_copy(off[:], bank[6][:, 0:1]))
            v.tensor_scalar(R[:, 0:CW], selp[:], off[:, 0:1], None, ALU.add).then_inc(s_R, 1)
            link(v.tensor_tensor(gstart[:], off[:], cst[:, C_GBASE:C_GBASE + 1], ALU.add))
            n = in_use(dv)

            def compare(j, k):
                dv.wait_ge(s_G, j - 1 + START)
                v.tensor_scalar(ge[:, k], cst[:, C_IOTA:C_IOTA + 384], of_slot(e320, j), gstart[:, 0:1],
                                ALU.add, ALU.is_ge).then_inc(s_ge, 1)

            def tokens(j, k):
                dv.wait_ge(s_G, j + 1 + START)
                dv.wait_ge(s_tok, j + START)
                for m in range(3):
                    prefix = bank[P_BANK[k][m]]
                    last = v.tensor_scalar(junk[:, m], prefix[:, 0:CW], cst[:, C_SLOT + m:C_SLOT + m + 1],
                                           prefix[:, CW:CW + 1], ALU.is_le, ALU.add,
                                           accum_out=tokf[:, bass.ds(3 * j + m, 1)])
                last.then_inc(s_tok, 1)

            compare(0, 0)
            dv.wait_ge(s_D, 1)
            v.tensor_copy(Dl[:], bank[7][:, 0:CW + 1]).then_inc(s_Dc, 1)
            with dv.Fori(0, E - 1, 2) as i:
                for k in range(2):
                    with dv.If(i + k + 1 < n):
                        compare(i + k + 1, 1 - k)
                    with dv.If(i + k < n):
                        tokens(i + k, k)

            steps = done[0]

            def expert(j, k):
                dv.wait_ge(s_gat[k], 24 * (j - k) + 48)
                v.tensor_scalar(ne1[:, k], xg[:, k, :, D], of_slot(elist, j), None, ALU.not_equal)
                v.tensor_tensor(wdiff[:, k], xg[:, k, :, D + 2], xg[:, k, :, D + 1], ALU.subtract).then_inc(s_v, 3)
                dv.wait_ge(s_v, steps + 6 * j + 3)
                v.tensor_tensor(wdiff[:, k], wdiff[:, k], ne1[:, k], ALU.mult).then_inc(s_v, 3)
                dv.wait_ge(s_v, steps + 6 * j + 6)
                dv.wait_ge(s_yc, j - 1 + START)
                v.tensor_tensor(wslot[:, k], wdiff[:, k], xg[:, k, :, D + 1], ALU.add)
                dv.wait_ge(s_sct[k], 24 * (j - k) + ZEROED)
                dv.wait_ge(s_tok, n + START)
                v.scalar_tensor_tensor(dst[:, k], ne1[:, k], float(N), tokf[:, bass.ds(3 * j, 3)],
                                       ALU.mult, ALU.add).then_inc(s_dst, 1)
                for hb in range(HB):
                    dv.wait_ge(s_es, 2 * j + hb + 1)
                    v.tensor_tensor(gue[:, hb], sile[:, hb], bank[U_BANK[hb]][:, 0:CAP], ALU.mult).then_inc(s_eg, 1)

            places(dv, n, expert)
            for b in range(B):
                q = slice(4 * b, 4 * b + 4)
                dv.wait_ge(s_yl[b // 2], 128)
                v.tensor_tensor(total[:, q, :], y[:, q, :], y[:, 4 * b + NT:4 * b + 4 + NT, :], ALU.add).then_inc(s_dv, 1)
                dv.wait_ge(s_dv, 4 * b + 1)
                dv.wait_ge(s_shc, b + 1)
                v.tensor_tensor(total[:, q, :], total[:, q, :], shared[:, q, :], ALU.add).then_inc(s_dv, 1)
                dv.wait_ge(s_dv, 4 * b + 2)
                for t in range(4 * b, 4 * b + 4):
                    last = v.bn_stats(bn[3][:, t, :], total[:, t, :])
                last.then_inc(s_dv, 1)
                dv.wait_ge(s_dv, 4 * b + 3)
                for t in range(4 * b, 4 * b + 4):
                    last = v.bn_aggr(mv[3][:, t, :], bn[3][:, t, :])
                last.then_inc(s_dv, 1)
                dv.wait_ge(s_dv, 4 * b + 4)
                negate_mean(3, b)
                variance(3, b)
            dv.wait_ge(s_n4, B)
            v.tensor_tensor(res[:, NT - 4:NT, :], total[:, NT - 4:NT, :], x1[:, NT - 4:NT, :], ALU.add).then_inc(s_fin, 1)

        @block.tensor
        def _(pe):
            t_ = nc.tensor

            def transpose_x(b):
                pe.wait_ge(s_xn, b + 1)
                if b == 0:
                    pe.wait_ge(s_const, 16)
                else:
                    pe.wait_ge(s_xtc, max(b - 1, 1)) if b >= 2 else None
                for t in range(4):
                    last = t_.transpose(bank[b % 2][:, 128 * t:128 * t + 128], xn[:, 4 * b + t, 0:D], ident)
                last.then_inc(s_xt, 1)

            def scores(b):
                pe.wait_ge(s_xtc, b + 1)
                if b >= 2:
                    pe.wait_ge(s_ex, 2 * (b - 1))
                for t in range(4):
                    xt = xnT[:, 4 * b + t, :]
                    last = t_.matmul(bank[2 + b % 2][:, 128 * t:128 * t + 128], xt, xt, start=True, stop=True)
                last.then_inc(s_sc, 1)

            def attend(b):
                pe.wait_ge(s_ex, 2 * (b + 1))
                if b >= 2:
                    pe.wait_ge(s_a2, b - 1)
                for t in range(4 * b, 4 * b + 4):
                    last = t_.matmul(attended(t), P[:, t, :], xn[:, t, :], start=True, stop=True)
                last.then_inc(s_pv, 1)

            def transpose_h(b):
                pe.wait_ge(s_h, b + 1)
                pe.wait_ge(s_htc, b - 1) if b >= 2 else pe.wait_ge(s_xtc, b + 3)
                for t in range(4):
                    last = t_.transpose(bank[b % 2][:, 128 * t:128 * t + 128], h[:, 4 * b + t, 0:D], ident)
                last.then_inc(s_ht, 1)

            def gate(b):
                pe.wait_ge(s_htc, b + 1)
                for t in range(4 * b, 4 * b + 4):
                    last = t_.matmul(bank[2][:, E * t:E * t + E], hT[:, 128 * t:128 * t + 128], gw[:],
                                     start=True, stop=True)
                return last

            transpose_x(0), transpose_x(1), scores(0), transpose_x(2), scores(1)
            attend(0), transpose_x(3), scores(2), attend(1), scores(3), attend(2)
            pe.wait_ge(s_w, 64)
            transpose_h(0), attend(3), transpose_h(1), gate(0), transpose_h(2), gate(1), transpose_h(3), gate(2)
            gate(3).then_inc(s_lg, 1)
            pe.wait_ge(s_wm, 1)
            for rp in range(2):
                last = t_.transpose(bank[7][:, 128 * rp:128 * rp + 128],
                                    wmP[:, rp, :, :].rearrange("p e c -> p (e c)"), ident)
            last.then_inc(s_kt, 1)
            pe.wait_ge(s_set, 2)
            t_.matmul(bank[5][:, 0:256], onesb[:], asg[:, :, :].rearrange("p t e -> p (t e)"), start=True, stop=True).then_inc(s_nct, 1)

            with pe.Fori(0, 4) as c:
                for k in range(SU):
                    sh, hb = k // HB, k % HB
                    xt = hT[:, bass.ds(c * 512, 512)]
                    pe.wait_ge(s_gu, c * SU + k - 1 + START)
                    t_.matmul(bank[k % 2][:], w1s[:, sh, 128 * hb:128 * hb + 128], xt, start=True, stop=True)
                    t_.matmul(bank[2 + k % 2][:], w3s[:, sh, 128 * hb:128 * hb + 128], xt,
                              start=True, stop=True).then_inc(s_up, 1)
                    pe.wait_ge(s_cnt, c * SU + k + 1)
                    t_.matmul(bank[6][:, 0:3], blockb[:], cnt[:], start=True, stop=True).then_inc(s_tot, 1)

            def down(c, t):
                for k in range(SU):
                    last = t_.matmul(down_bank(c)[:, 128 * t:128 * t + 128], gu[:, SU * c + k, 128 * t:128 * t + 128],
                                     w2s[:, k, :], start=k == 0, stop=k == SU - 1)
                return last

            block_ = cst[:, C_BLOCK:C_BLOCK + 128]
            down(0, 0)
            pe.wait_ge(s_eq, 1)
            t_.matmul(bank[6][:, 0:2], block_, tot[:], start=True, stop=True)
            t_.matmul(bank[6][:, 2:4], beforef, tot[:], start=True, stop=True).then_inc(s_eqt, 1)
            down(0, 1)
            pe.wait_ge(s_sl, 1)
            t_.matmul(bank[6][:, 0:2], beforef, tot[:], start=True, stop=True).then_inc(s_slt, 1)
            pe.wait_ge(s_R, 1)
            t_.matmul(bank[7][:, 0:CW + 1], deltah[:], R[:], start=True, stop=True).then_inc(s_D, 1)
            down(0, 2)
            down(0, 3).then_inc(s_dn, 1)
            n = in_use(pe)
            pe.wait_ge(s_Dc, 1)

            def prefixes(j, k):
                pe.wait_ge(s_ge, j + 1)
                pe.wait_ge(s_tok, j - 1 + START)
                for m in range(3):
                    last = t_.matmul(bank[P_BANK[k][m]][:, 0:CW + 1], ge[:, k, 128 * m:128 * m + 128], Dl[:],
                                     start=True, stop=True)
                last.then_inc(s_G, 1)

            places(pe, n, prefixes)

            def expert(j, k):
                pe.wait_ge(s_gat[k], 24 * (j - k) + 48)
                pe.wait_ge(s_tok, n + START)
                pe.wait_ge(s_gtc, j + START)
                for m, rows in enumerate(SLOT_ROWS):
                    last = t_.transpose(bank[0][:, 128 * m:128 * m + rows], xg[0:rows, k, m, 0:D],
                                        ident[0:rows, 0:rows])
                last.then_inc(s_gt, 1)
                pe.wait_ge(s_wl[k], 24 * (j - k) + 48)
                pe.wait_ge(s_gtc, j + 1 + START)
                pe.wait_ge(s_eg, 2 * j + START)
                for hb in range(HB):
                    t_.matmul(bank[G_BANK[hb]][:, 0:CAP], w1e[:, k, 128 * hb:128 * hb + 128], xgT[:, k], start=True, stop=True)
                    t_.matmul(bank[U_BANK[hb]][:, 0:CAP], w3e[:, k, 128 * hb:128 * hb + 128], xgT[:, k],
                              start=True, stop=True).then_inc(s_eu, 1)
                pe.wait_ge(s_eg, 2 * j + 2 + START)
                pe.wait_ge(s_yc, j + START)
                for m, rows in enumerate(SLOT_ROWS):
                    for hb in range(HB):
                        last = t_.matmul(bank[6][0:rows, 128 * m:128 * m + 128], gue[:, hb, 128 * m:128 * m + rows],
                                         w2e[:, k, hb, :], start=hb == 0, stop=hb == HB - 1)
                last.then_inc(s_ed, 1)

            places(pe, n, expert)
            for c in range(1, 4):
                pe.wait_ge(s_shc, c - 1 if c > 1 else 1)
                for t in range(4):
                    last = down(c, t)
                last.then_inc(s_dn, 1)


_INS = ["L0_attn_x", "L0_ffn_gate_w", "L0_ffn_gate_b", "L0_ffn_ew1", "L0_ffn_ew3", "L0_ffn_ew2",
        "L0_ffn_sw1", "L0_ffn_sw3", "L0_ffn_sw2"]


def kernel(**inputs):
    import numpy as _np
    import concourse.bacc as _bacc
    from concourse import mybir as _mybir
    from concourse.bass_utils import run_bass_kernel_spmd as _run

    nc = _bacc.Bacc("TRN2", target_bir_lowering=False, num_devices=1)
    arrays, args = {}, []
    for name in _INS:
        a = _np.ascontiguousarray(inputs[name])
        if name == "L0_attn_x":
            a = a.reshape(N, D)
        arrays[f"in_{name}"] = a
        args.append(nc.dram_tensor(f"in_{name}", a.shape, _mybir.dt.from_np(a.dtype), kind="ExternalInput").ap())
    arrays["in_constants"] = constants()
    args.append(nc.dram_tensor("in_constants", (128, C_ALL), _mybir.dt.float32, kind="ExternalInput").ap())
    args.append(nc.dram_tensor("out_0", (N, D), _mybir.dt.float32, kind="ExternalOutput").ap())
    build(nc, *args)
    r = _run(nc, [arrays], core_ids=[0])
    return r.results[0]["out_0"].reshape(B, T, D)
```

```python
from contextlib import ExitStack

import concourse.bass as bass
import numpy as np
from concourse import mybir

B, T, D, E, H, S = 4, 512, 128, 16, 256, 2
N = B * T
NT = N // 128
CAP = 320
CH = 8
CW = N // CH
HB = H // 128
SLOT_ROWS = (128, 128, 64)
HW = 132
EPS = 1e-5
UNASSIGNED = -1.0e38
ROUNDS = 8
SU = S * HB
ZEROED = 64
AHEAD = 4
SCALED = (1, 2)
UNROLLED = 8
BY_SCALAR = 2
START = 4

C_ID, C_BLOCK, C_BEFORE, C_DELTA = 0, 128, 256, 384
C_IOTA = 512
C_CAND = C_IOTA + 384
C_STEP = C_CAND + 3 * (2 * ROUNDS)
C_FIRST = C_STEP + 2 * ROUNDS
C_EIX = C_FIRST + 3
C_PLACE = C_EIX + E
C_SPREAD = C_PLACE + 1
C_SLOT = C_SPREAD + E
C_GBASE = C_SLOT + 3
C_CBASE = C_GBASE + 1
C_PAD = C_CBASE + 1
C_ALL = C_PAD + HW


def constants():
    c = np.zeros((128, C_ALL), np.float32)
    p = np.arange(128)
    c[:, C_ID:C_ID + 128] = np.eye(128)
    same = p[:, None] // CH == p[None, :] // CH
    c[:, C_BLOCK:C_BLOCK + 128] = same
    c[:, C_BEFORE:C_BEFORE + 128] = same & (p[:, None] < p[None, :])
    c[:, C_DELTA:C_DELTA + 128] = np.eye(128) - np.eye(128, k=1)
    c[:, C_IOTA:C_IOTA + 384] = np.arange(384)
    for k in range(2 * ROUNDS):
        c[:, C_STEP + k] = 4 ** (ROUNDS - 1 - k % ROUNDS) * (65536 if k < ROUNDS else 1)
    for half_ in range(2):
        for k in range(ROUNDS):
            r = half_ * ROUNDS + k
            following = c[0, C_STEP + r + 1] * np.arange(1, 4) if k < ROUNDS - 1 else np.zeros(3)
            c[:, C_CAND + 3 * r:C_CAND + 3 * r + 3] = following - c[0, C_STEP + r]
    c[:, C_FIRST:C_FIRST + 3] = 4 ** (ROUNDS - 1) * np.arange(1, 4)
    c[:, C_EIX:C_EIX + E] = np.arange(E)
    c[:, C_PLACE] = p // CH + 1
    c[:, C_SPREAD:C_SPREAD + E] = p[:, None] == CH * np.arange(E)
    for k in range(3):
        c[:, C_SLOT + k] = p + 128 * k
    c[:, C_GBASE] = CAP * (p // CH)
    c[:, C_CBASE] = CW * (p % CH)
    c[:, C_PAD + D] = -1.0
    return c


def build(nc, x, gate_w, gate_b, ew1, ew3, ew2, sw1, sw3, sw2, consts, out):
    f32, bf16, f16, i32 = mybir.dt.float32, mybir.dt.bfloat16, mybir.dt.float16, mybir.dt.int32
    ALU, ACT, AX = mybir.AluOpType, mybir.ActivationFunctionType, mybir.AxisListType.X
    v, s_, g_ = nc.vector, nc.scalar, nc.gpsimd

    ctx = ExitStack()
    with ctx:
        def sb(name, shape, dt=f32):
            return ctx.enter_context(nc.sbuf_tensor(name, shape, dt))

        def sem(name):
            return ctx.enter_context(nc.semaphore(name))

        htab = nc.dram_tensor("htab", [N + 1, HW], f32).ap()
        ytab = nc.dram_tensor("ytab", [2 * N, D], f32).ap()

        def tiled(ap):
            v = ap.rearrange("(a q rp r2) d -> r2 rp q a d", q=64, rp=2, r2=2)
            return [[v[r2][rp] for rp in range(2)] for r2 in range(2)]

        def tiles(buf):
            v = buf[:, :, :].rearrange("p (a rp) d -> p rp a d", rp=2)
            return [[v[64 * r2:64 * r2 + 64, rp] for rp in range(2)] for r2 in range(2)]

        cst = sb("cst", [128, C_ALL])
        xs_in = sb("x_in", [128, NT, D])
        xn = sb("xn", [128, NT, D + 2])
        xnT = sb("xnT", [128, NT, 128])
        P = sb("P", [128, NT, 128])
        x1 = sb("x1", [128, NT, D])
        h = sb("h", [128, NT, HW])
        hT = sb("hT", [128, NT * 128])
        ones = sb("ones", [128, 2])
        zeros = sb("zeros", [128, 512])
        idle = sb("idle", [128, 512], bf16)
        bn = [sb(f"bn{k}", [128, NT, 6]) for k in range(4)]
        mv = [sb(f"mv{k}", [128, NT, 2]) for k in range(4)]
        var = [sb(f"var{k}", [128, NT]) for k in range(4)]
        rstd = [sb(f"rstd{k}", [128, NT]) for k in range(4)]
        nmean = [sb(f"nmean{k}", [128, NT]) for k in range(4)]
        shift = [sb(f"shift{k}", [128, NT]) for k in range(4)]
        lsum = sb("lsum", [128, NT])
        lsq = sb("lsq", [128, NT])
        half = sb("half", [128, 4])
        lg = sb("lg", [128, NT, E])
        mx = sb("mx", [128, NT])
        ex = sb("ex", [128, NT, E])
        sc = sb("sc", [128, NT, E])
        inv = sb("inv", [128, NT])
        top = sb("top", [128, NT, 8])
        pick = sb("pick", [128, NT, 8], mybir.dt.uint32)
        oh1 = sb("oh1", [128, NT, E])
        oh2 = sb("oh2", [128, NT, E])
        asg = sb("asg", [128, NT, E], bf16)
        bias = sb("bias", [128, E])
        gw = sb("gw", [128, E])
        wmP = sb("wmP", [128, 2, E, CH])
        onesb = sb("onesb", [128, 128], bf16)
        blockb = sb("blockb", [128, 128], bf16)
        beforef = cst[:, C_BEFORE:C_BEFORE + 128]
        deltah = sb("deltah", [128, 128], f16)
        ident = cst[:, C_ID:C_ID + 128]
        act = sb("act", [128, E])
        rank = sb("rank", [128, E])
        used = sb("used", [128, E])
        at_place = sb("at_place", [128, E])
        lval = sb("lval", [128, 1])
        lspread = sb("lspread", [128, E], bf16)
        elist = sb("elist", [128, E])
        e320 = sb("e320", [128, E + AHEAD])
        elist_i = sb("elist_i", [128, E + 1], i32)
        K = sb("K", [128, CW])
        m32 = sb("m32", [128, CW], i32)
        s32 = sb("s32", [128, CW], i32)
        part = sb("part", [128, 2, CW], i32)
        hi = sb("hi", [128, CW])
        lo = sb("lo", [128, CW])
        key2 = sb("key2", [128, CW])
        assigned = sb("assigned", [128, CW])
        junk = sb("junk", [128, 3, CW])
        above = sb("above", [128, CW])
        cand = sb("cand", [128, 3])
        cnt = sb("cnt", [128, 3], bf16)
        step = sb("step", [128, 1])
        moves = sb("moves", [128, 3, 4])
        tot = sb("tot", [128, 2])
        ties = sb("ties", [128, CW])
        aboves = sb("aboves", [128, CW])
        tied = sb("tied", [128, CW])
        rem = sb("rem", [128, 1])
        offs = sb("offs", [128, 2])
        off = sb("off", [128, 1])
        gstart = sb("gstart", [128, 1])
        R = sb("R", [128, CW + 1], f16)
        Dl = sb("Dl", [128, CW + 1], f16)
        w1s = sb("w1s", [128, S, H])
        w3s = sb("w3s", [128, S, H])
        w2s = sb("w2s", [128, S * HB, D])
        w2m = sb("w2m", [128, S * HB, D])
        sil = sb("sil", [128, 2, 512])
        upc = sb("upc", [128, 2, 512])
        gu = sb("gu", [128, 4 * SU, 512])
        ge = sb("ge", [128, 2, 384], f16)
        tokf = sb("tokf", [128, 3 * (E + AHEAD + 1)])
        idx = sb("idx", [128, AHEAD, 3], i32)
        ne1 = sb("ne1", [128, AHEAD, 3])
        dst = sb("dst", [128, AHEAD, 3], i32)
        wdiff = sb("wdiff", [128, AHEAD, 3])
        wslot = sb("wslot", [128, AHEAD, 3])
        xg = sb("xg", [128, AHEAD, 3, HW])
        w1e = sb("w1e", [128, AHEAD, H])
        w3e = sb("w3e", [128, AHEAD, H])
        w2e = sb("w2e", [128, AHEAD, HB, D])
        xgT = sb("xgT", [128, 2, CAP])
        sile = sb("sile", [128, HB, CAP])
        gue = sb("gue", [128, HB, CAP])
        ye = sb("ye", [128, 2, 3, D])
        y = sb("y", [128, 2 * NT, D])
        total = sb("total", [128, NT, D])
        res = xs_in

        bank = [ctx.enter_context(nc.psum_tensor(f"bank{i}", [128, 512], f32)) for i in range(8)]

        P_BANK = ((0, 1, 2), (3, 5, 6))
        G_BANK, U_BANK = (1, 2), (3, 5)
        SG_BANK, SU_BANK = (0, 1), (3, 5)

        GATE_PARTS, GATE_BANK = ((0, 3), (3, 4)), (2, 4)

        SUM_BANK = (4, 0, 7, 1)

        def group(b, last=False):
            return slice(8 * (b % 2) + b // 2, 8 * (b % 2) + 8, 2) if last else slice(4 * b, 4 * b + 4)

        def group_tiles(b, last=False):
            return range(NT)[group(b, last)]

        def attended_pair(t):
            return bank[4 + (t // 2) % 4][:, 0:2 * (D + 2)].rearrange("p (t d) -> p t d", t=2)

        def attended(t):
            return attended_pair(t)[:, t % 2, :]

        def of_slot(ap, j):
            return ap[:, bass.ds(j, 1)]

        def load_x(eng, r2):
            for half_ in range(2):
                a = CH // 2 * half_
                for rp in range(2):
                    eng.dma_start(tiles(xs_in)[r2][rp][:, a:a + CH // 2], tiled(x)[r2][rp][:, a:a + CH // 2]).then_inc(s_x[half_], 16)

        s_id, s_const, s_w, s_bias = sem("identity_loaded"), sem("constants_loaded"), sem("weights_loaded"), sem("bias_loaded")
        s_x = [sem("x_first_half_loaded"), sem("x_second_half_loaded")]
        s_zero, s_pad, s_hw = sem("zeros_set"), sem("pad_row_written"), sem("htab_written")
        s_half, s_set = sem("half_set"), sem("fills_set")
        s_var = [sem(f"var{k}_ready") for k in range(4)]
        s_r = [sem(f"rstd{k}_ready") for k in range(4)]
        s_sh1, s_idle, s_xnv = sem("attn_shift_ready"), sem("idle_set"), sem("xn_by_vector_ready")
        s_hv, s_scaled = sem("last_h_ready"), sem("attention_scaled")
        s_last = sem("last_tiles_ready")
        s_fin4 = sem("last_result_ready")
        s_xn, s_xt, s_xtc = sem("xn_ready"), sem("x_transposed"), sem("xT_copied")
        s_sc, s_ex, s_pv, s_x1 = sem("scores_ready"), sem("probs_ready"), sem("attn_ready"), sem("x1_ready")
        s_h, s_ht, s_htc, s_lg = sem("h_ready"), sem("h_transposed"), sem("hT_copied"), sem("logits_ready")
        s_lmx, s_gex = sem("logits_centred"), sem("gate_exp_ready")
        s_h1 = sem("choices_in_h")
        s_nct = sem("expert_counts_ready")
        s_lval, s_spread, s_list = sem("list_values_ready"), sem("list_spread"), sem("list_ready")
        s_wm, s_kt = sem("masked_logits_ready"), sem("expert_major_ready")
        s_cnt, s_tot = sem("counts_ready"), sem("totals_ready")
        s_up, s_sil, s_gu, s_w2m = sem("shared_up_done"), sem("shared_silu_done"), sem("shared_gu_done"), sem("mean_w2_ready")
        s_eq, s_eqt, s_R, s_D, s_Dc = (sem("ties_counted"), sem("tie_totals"), sem("rows_ready"), sem("differences_ready"),
                                       sem("differences_copied"))
        s_ge, s_G, s_tok = sem("slots_compared"), sem("prefix_rows_ready"), sem("tokens_of_slots")
        s_wl = [sem(f"expert_weights{k}_loaded") for k in range(AHEAD)]
        s_gat = [sem(f"rows{k}_gathered") for k in range(AHEAD)]
        s_sct = [sem("rows_scattered_even"), sem("rows_scattered_odd")]
        s_idx, s_dst = sem("index_copied"), sem("destinations_ready")
        s_gt, s_gtc = sem("gathered_transposed"), sem("gathered_T_copied")
        s_eu, s_es, s_eg, s_ed, s_yc = (sem("expert_up_done"), sem("expert_silu_done"), sem("expert_gu_done"),
                                        sem("expert_down_done"), sem("expert_out_copied"))
        s_y1 = sem("expert_first_tile_copied")
        s_yl = [sem("y_of_even_tiles_loaded"), sem("y_of_odd_tiles_loaded")]
        s_y3 = sem("last_choices_added")
        s_sum = sem("result_summed")
        s_n4, s_fin, s_out = sem("result_normed"), sem("result_ready"), sem("out_written")
        s_v, s_dv = sem("vector_step"), sem("vector_end_step")
        counts_from_start = (s_sil, s_gu, s_gt, s_dst, s_yc, s_y1, s_gtc, s_eg, s_ed, s_tok, s_G)

        def places(eng, n, body, start=0):
            def from_(i, k):
                with eng.If(i + k < n):
                    body(i + k, k % AHEAD)
                    if k + 1 < UNROLLED:
                        from_(i, k + 1)

            with eng.Fori(start, E - UNROLLED + 1 + start, UNROLLED) as i:
                from_(i, 0)

        def loaded(j, k):
            return 48 // AHEAD * (j - k) + 48

        def scattered(eng, n):
            eng.wait_ge(s_sct[0], 48 * ((n + 1) // 2) + ZEROED)
            eng.wait_ge(s_sct[1], 48 * (n // 2) + ZEROED)

        def load_results(eng, r2):
            for rp in range(2):
                eng.dma_start(tiles(y)[r2][rp], tiled(ytab[:, :])[r2][rp]).then_inc(s_yl[rp], 16)

        def store(eng, g, r2):
            eng.wait_ge(s_fin, g + 1) if g < B - 1 else eng.wait_ge(s_fin4, 1)
            a = group(g, True).start // 2
            eng.dma_start(tiled(out)[r2][g // 2][:, a:a + 4], tiles(res)[r2][g // 2][:, a:a + 4]).then_inc(s_out, 16)

        def in_use(eng):
            return eng.value_load(elist_i[0:1, E:E + 1], min_val=2, max_val=E)

        block = ctx.enter_context(nc.Block())

        @block.sync
        def _(sp):
            load_x(sp, 0)
            for s in counts_from_start:
                sp.sem_inc(s, START)
            sp.dma_start(cst[:, 128:C_ALL], consts[:, 128:C_ALL]).then_inc(s_const, 16)
            sp.dma_start(gw[:], gate_w).then_inc(s_w, 16)
            sp.dma_start(w1s[:], sw1.rearrange("s d h -> d s h")).then_inc(s_w, 16)
            sp.dma_start(w3s[:], sw3.rearrange("s d h -> d s h")).then_inc(s_w, 16)
            sp.dma_start(w2s[:], sw2.rearrange("s (k p) d -> p (s k) d", p=128)).then_inc(s_w, 16)
            sp.dma_start(bias[:], gate_b.rearrange("(o e) -> o e", o=1).broadcast_to([128, E])).then_inc(s_bias, 16)
            sp.wait_ge(s_const, 16)
            sp.dma_start(htab[N:N + 1, :], cst[0:1, C_PAD:C_PAD + HW]).then_inc(s_pad, 16)
            sp.wait_ge(s_h1, 1)
            for r2 in range(2):
                for rp in range(2):
                    sp.dma_start(tiled(htab[0:N, :])[r2][rp], tiles(h)[r2][rp]).then_inc(s_hw, 16)
            sp.wait_ge(s_list, 1)
            n = in_use(sp)

            def load_weights(j, k):
                e = sp.value_load(elist_i[0:1, bass.ds(j, 1)], min_val=0, max_val=E - 1)
                sp.wait_ge(s_ed, j + 1 - AHEAD + START)
                sp.dma_start(w1e[:, k], ew1[bass.ds(e, 1)].rearrange("o d h -> d (o h)")).then_inc(s_wl[k], 16)
                sp.dma_start(w3e[:, k], ew3[bass.ds(e, 1)].rearrange("o d h -> d (o h)")).then_inc(s_wl[k], 16)
                sp.dma_start(w2e[:, k], ew2[bass.ds(e, 1)].rearrange("o (k p) d -> p (o k) d", p=128)).then_inc(s_wl[k], 16)

            places(sp, n, load_weights)
            scattered(sp, n)
            load_results(sp, 0)
            for g in range(B - 1):
                store(sp, g, 0), store(sp, g, 1)
            store(sp, B - 1, 0)
            sp.wait_ge(s_out, 128)

        @block.gpsimd
        def _(pool):
            pool.memset(half[:], -0.5).then_inc(s_half, 1)
            pool.memset(zeros[:], 0.0).then_inc(s_zero, 1)
            g_.memset(xn[:, :, D:D + 2], 1.0)
            g_.memset(P[:], 0.0).then_inc(s_set, 1)
            pool.wait_ge(s_half, 1)

            def normalise(k, b, shifted):
                q = group(b, k == 3)
                seen = (3 if k == 3 else 2) * b
                pool.wait_ge(s_var[k], b + 1)
                g_.tensor_tensor(rstd[k][:, q], var[k][:, q], half[:], ALU.pow).then_inc(s_r[k], 1)
                if shifted:
                    pool.wait_ge(s_r[k], seen + 1)
                    g_.tensor_tensor(shift[k][:, q], nmean[k][:, q], rstd[k][:, q], ALU.mult).then_inc(s_r[k], 1)

            for b in range(B):
                normalise(0, b, b < BY_SCALAR)
            for b in range(B + 1):
                if b < B:
                    normalise(1, b, False)
                if b:
                    normalise(2, b - 1, True)
            pool.wait_ge(s_r[1], B)
            g_.tensor_tensor(shift[1][:], mv[1][:, :, 0], rstd[1][:], ALU.mult).then_inc(s_sh1, 1)
            pool.wait_ge(s_const, 16)
            g_.tensor_copy(blockb[:], cst[:, C_BLOCK:C_BLOCK + 128])
            g_.tensor_copy(deltah[:], cst[:, C_DELTA:C_DELTA + 128])
            g_.memset(onesb[:], 1.0)
            g_.memset(ones[:], 1.0).then_inc(s_set, 1)
            pool.wait_ge(s_zero, 1)
            for k in range(8):
                pool.dma_start(ytab[N // 4 * k:N // 4 * (k + 1), :].rearrange("(p r) d -> p (r d)", p=128),
                               zeros[:, :]).then_inc(s_sct[k % 2], 16)
            g_.memset(xg[:], 0.0)
            with pool.Fori(0, 4) as c:
                for k in range(SU):
                    pool.wait_ge(s_sil, c * SU + k + 1 + START)
                    g_.tensor_tensor(gu[:, bass.ds(c * SU + k, 1), :].rearrange("p o n -> p (o n)"), sil[:, k % 2], upc[:, k % 2],
                                     ALU.mult).then_inc(s_gu, 1)
            pool.wait_ge(s_sct[1], ZEROED)
            pool.wait_ge(s_pad, 16)
            pool.wait_ge(s_list, 1)
            n = in_use(pool)
            last_token, last_result = pool.to_reg(N), pool.to_reg(2 * N - 1)

            def gather(j, k):
                pool.wait_ge(s_gt, j + 1 - AHEAD + START)
                pool.wait_ge(s_dst, j + 1 - AHEAD + START)
                pool.wait_ge(s_tok, j + 1 + START)
                g_.tensor_copy(idx[:, k], tokf[:, bass.ds(3 * j, 3)]).then_inc(s_idx, 1)
                pool.wait_ge(s_hw, 64)
                pool.wait_ge(s_idx, j + 1)
                for m, rows in enumerate(SLOT_ROWS):
                    g_.indirect_dma_start(
                        out=xg[0:rows, k, m, :], out_offset=None, in_=htab[:, :],
                        in_offset=bass.IndirectOffsetOnAxis(ap=idx[0:rows, k, m:m + 1], axis=0),
                        bounds_check=last_token, oob_is_err=False).then_inc(s_gat[k], 16)

            def scatter(j, k):
                this = pool.compute_val(j + 1 + START)
                pool.wait_ge(s_sct[0], ZEROED)
                pool.wait_ge(s_dst, this)
                pool.wait_ge(s_y1, this)
                for m, rows in enumerate(SLOT_ROWS):
                    if m == 1:
                        pool.wait_ge(s_sct[1], ZEROED)
                        pool.wait_ge(s_yc, this)
                    g_.indirect_dma_start(
                        out=ytab[:, :], out_offset=bass.IndirectOffsetOnAxis(ap=dst[0:rows, k, m:m + 1], axis=0),
                        in_=ye[0:rows, k % 2, m, :], in_offset=None,
                        bounds_check=last_result, oob_is_err=False).then_inc(s_sct[k % 2], 16)

            gather(0, 0), gather(1, 1)
            for k in range(2, AHEAD):
                with pool.If(n > k):
                    gather(k, k)
            with pool.If(n > AHEAD):
                gather(AHEAD, 0)

            def scatter_and_gather(j, k):
                scatter(j, k)
                with pool.If(j + AHEAD + 1 < n):
                    gather(j + AHEAD + 1, (k + 1) % AHEAD)

            places(pool, n, scatter_and_gather)
            pool.wait_ge(s_sh1, 1)
            for b in range(B):
                normalise(3, b, True)
                q = group(b, True)
                pool.wait_ge(s_r[3], 3 * b + 2)
                g_.tensor_tensor(shift[3][:, q], shift[3][:, q], shift[1][:, q], ALU.subtract).then_inc(s_r[3], 1)

        @block.scalar
        def _(ac):
            load_x(ac, 1)
            ac.dma_start(cst[:, 0:128], consts[:, 0:128]).then_inc(s_id, 16)

            def norm(k, t, dst_, src):
                return s_.activation(dst_, src, ACT.Identity, bias=shift[k][:, t:t + 1], scale=rstd[k][:, t:t + 1])

            def norm_x(b):
                ac.wait_ge(s_r[0], 2 * b + 2)
                for t in range(4 * b, 4 * b + 4):
                    last = norm(0, t, xn[:, t, 0:D], xs_in[:, t, :])
                last.then_inc(s_xn, 1)

            def copy_xT(b):
                ac.wait_ge(s_xt, b + 1)
                s_.activation(xnT[:, 4 * b:4 * b + 4, :], bank[b % 2][:, :], ACT.Identity).then_inc(s_xtc, 1)

            def exponentials(b):
                ac.wait_ge(s_sc, b + 1)
                ac.wait_ge(s_set, 1)
                sc4 = bank[2 + b % 2][:, :].rearrange("p (t k) -> p t k", t=4)
                for r2 in range(2):
                    q = slice(64 * r2, 64 * r2 + 64)
                    s_.activation(P[q, 4 * b:4 * b + 4, q], sc4[q, :, q], ACT.Exp, scale=float(D) ** -0.5).then_inc(s_ex, 1)

            def norm_h(b):
                ac.wait_ge(s_r[2], 2 * b + 2)
                for t in range(4 * b, 4 * b + 4):
                    last = norm(2, t, h[:, t, 0:D], x1[:, t, :])
                last.then_inc(s_h, 1)

            def copy_hT(b):
                ac.wait_ge(s_ht, b + 1)
                s_.activation(hT[:, 512 * b:512 * b + 512], bank[b % 2][:, :], ACT.Identity).then_inc(s_htc, 1)

            norm_x(0), norm_x(1), copy_xT(0), copy_xT(1), exponentials(0), exponentials(1), copy_xT(2)
            copy_xT(3), exponentials(2), exponentials(3)

            def gate_exponentials(part_):
                ac.wait_ge(s_lmx, part_ + 1)
                q = slice(4 * GATE_PARTS[part_][0], 4 * GATE_PARTS[part_][1])
                s_.activation(ex[:, q, :], sc[:, q, :], ACT.Exp).then_inc(s_gex, 1)

            ac.wait_ge(s_w, 64)
            s_.activation(w2m[:], w2s[:], ACT.Identity, scale=1.0 / S).then_inc(s_w2m, 1)
            def scale_attended(b):
                ac.wait_ge(s_r[1], b + 1)
                for t in group_tiles(b):
                    ins = s_.activation(x1[:, t, :], attended(t)[:, 0:D], ACT.Identity, scale=rstd[1][:, t:t + 1])
                    if t % 2:
                        ins.then_inc(s_scaled, 1)

            scale_attended(1), norm_h(0), scale_attended(2), copy_hT(0), norm_h(1), copy_hT(1)
            norm_h(2), copy_hT(2), copy_hT(B - 1)
            gate_exponentials(0)
            gate_exponentials(1)
            s_.preload_act_table(ACT.Silu)
            with ac.Fori(0, 4) as c:
                for k in range(SU):
                    ac.wait_ge(s_up, c * SU + k + 1)
                    ac.wait_ge(s_gu, c * SU + k - 1 + START)
                    s_.activation(sil[:, k % 2], bank[SG_BANK[k % 2]][:], ACT.Silu)
                    s_.activation(upc[:, k % 2], bank[SU_BANK[k % 2]][:], ACT.Identity).then_inc(s_sil, 1)

            n = in_use(ac)

            def copy_gathered(j, k):
                ac.wait_ge(s_gt, j + 1 + START)
                s_.activation(xgT[:, k % 2], bank[0][:, 0:CAP], ACT.Identity).then_inc(s_gtc, 1)

            def hidden(j, k):
                for hb in range(HB):
                    ac.wait_ge(s_eu, 2 * j + hb + 1)
                    s_.activation(sile[:, hb], bank[G_BANK[hb]][:, 0:CAP], ACT.Silu).then_inc(s_es, 1)

            def weigh(j, k):
                ac.wait_ge(s_ed, j + 1 + START)
                ac.wait_ge(s_sct[k % 2], 24 * (j - k % 2) + ZEROED)
                ac.wait_ge(s_dst, j + 1 + START)
                for m, rows in enumerate(SLOT_ROWS):
                    last = s_.activation(ye[0:rows, k % 2, m], bank[6][0:rows, 128 * m:128 * m + 128], ACT.Identity,
                                         scale=wslot[0:rows, k, m:m + 1])
                    if m == 0:
                        last.then_inc(s_y1, 1)
                last.then_inc(s_yc, 1)

            copy_gathered(0, 0)

            def expert(j, k):
                hidden(j, k)
                with ac.If(j + 1 < n):
                    copy_gathered(j + 1, (k + 1) % AHEAD)
                weigh(j, k)

            places(ac, n, expert)
            scattered(ac, n)
            load_results(ac, 1)
            for b in range(B - 1):
                ac.wait_ge(s_r[3], 3 * b + 3)
                for i, t in enumerate(group_tiles(b, True)):
                    last = norm(3, t, total[:, t, :], bank[SUM_BANK[b]][:, 128 * i:128 * i + 128])
                last.then_inc(s_n4, 1)
            ac.wait_ge(s_r[3], 3 * B)
            for i, t in enumerate(group_tiles(B - 1, True)):
                ac.wait_ge(s_last, i + 1)
                last = s_.activation(res[:, t, :], total[:, t, :], ACT.Identity, bias=shift[3][:, t:t + 1])
            last.then_inc(s_fin4, 1)
            store(ac, B - 1, 1)

        @block.vector
        def _(dv):
            done = [0]

            def link(ins):
                done[0] += 1
                ins.then_inc(s_v, 1)
                dv.wait_ge(s_v, done[0])

            def mark(ins):
                done[0] += 1
                ins.then_inc(s_v, 1)
                return done[0]

            ended = [0]

            def end_link(ins):
                ended[0] += 1
                ins.then_inc(s_dv, 1)
                dv.wait_ge(s_dv, ended[0])

            def stats(k, b, src):
                for i, t in enumerate(group_tiles(b, k == 3)):
                    last = v.bn_stats(bn[k][:, t, :], src(i, t))
                wait = end_link if k == 3 else link
                wait(last)
                for t in group_tiles(b, k == 3):
                    last = v.bn_aggr(mv[k][:, t, :], bn[k][:, t, :])
                wait(last)
                q = group(b, k == 3)
                if k != 1:
                    v.tensor_scalar(nmean[k][:, q], mv[k][:, q, 0], -1.0, None, ALU.mult)
                    v.tensor_scalar(var[k][:, q], mv[k][:, q, 1], EPS, None, ALU.add).then_inc(s_var[k], 1)

            def over_tiles(ap, nt):
                return ap.rearrange("p (o e) -> p o e", o=1).broadcast_to([128, nt, E])

            v.memset(idle[:], 0.0).then_inc(s_idle, 1)
            for b in range(B):
                dv.wait_ge(s_x[b // 2], 64)
                stats(0, b, lambda i, t: xs_in[:, t, :])
            for b in range(BY_SCALAR, B):
                dv.wait_ge(s_r[0], BY_SCALAR + b + 1)
                for t in group_tiles(b):
                    last = v.tensor_scalar(xn[:, t, 0:D], xs_in[:, t, :], mv[0][:, t, 0:1], rstd[0][:, t:t + 1],
                                           ALU.subtract, ALU.mult)
                last.then_inc(s_xnv, 1)
            def residual_stream(b, half_):
                if b in SCALED:
                    q = slice(4 * b + 2 * half_, 4 * b + 2 * half_ + 2)
                    dv.wait_ge(s_scaled, 2 * (b - SCALED[0]) + half_ + 1)
                    return v.tensor_tensor(x1[:, q, :], x1[:, q, :], xs_in[:, q, :], ALU.add)
                for t in group_tiles(b)[2 * half_:2 * half_ + 2]:
                    last = v.scalar_tensor_tensor(x1[:, t, :], attended(t)[:, 0:D], rstd[1][:, t:t + 1], xs_in[:, t, :],
                                                  ALU.mult, ALU.add)
                return last

            for b in range(B + 1):
                if b < B:
                    q = group(b)
                    dv.wait_ge(s_pv, b + 1)
                    for t in (4 * b, 4 * b + 2):
                        last = v.tensor_copy(lsum[:, t:t + 2], attended_pair(t)[:, :, D])
                    copied = mark(last)
                    for t in group_tiles(b):
                        last = v.bn_stats(bn[1][:, t, :], attended(t)[:, 0:D])
                    counted = mark(last)
                    dv.wait_ge(s_v, copied)
                    v.scalar_tensor_tensor(lsq[:, q], lsum[:, q], EPS * 16, lsum[:, q], ALU.mult, ALU.mult)
                if b:
                    dv.wait_ge(s_r[1], b)
                    residual_stream(b - 1, 0)
                if b < B:
                    dv.wait_ge(s_v, counted)
                    for t in group_tiles(b):
                        last = v.bn_aggr(mv[1][:, t, :], bn[1][:, t, :])
                    averaged = mark(last)
                if b:
                    residual_stream(b - 1, 1).then_inc(s_x1, 1)
                if b < B:
                    dv.wait_ge(s_v, averaged)
                    v.tensor_tensor(var[1][:, q], lsq[:, q], mv[1][:, q, 1], ALU.add).then_inc(s_var[1], 1)
                if b:
                    dv.wait_ge(s_x1, b)
                    stats(2, b - 1, lambda i, t: x1[:, t, :])
            dv.wait_ge(s_r[2], 2 * B - 1)
            for t in group_tiles(B - 1):
                last = v.tensor_scalar(h[:, t, 0:D], x1[:, t, :], mv[2][:, t, 0:1], rstd[2][:, t:t + 1],
                                       ALU.subtract, ALU.mult)
            last.then_inc(s_hv, 1)
            dv.wait_ge(s_bias, 16)
            wrote = {}

            def part_of(part_):
                b0, b1 = GATE_PARTS[part_]
                q = slice(4 * b0, 4 * b1)
                nt = 4 * (b1 - b0)
                return q, bank[GATE_BANK[part_]][:, 0:E * nt].rearrange("p (t e) -> p t e", e=E), \
                    lambda ap: ap[:, q].rearrange("p (t o) -> p t o", o=1).broadcast_to([128, nt, E])

            def largest(part_):
                q, logits, over_experts = part_of(part_)
                dv.wait_ge(s_lg, GATE_PARTS[part_][1])
                wrote["largest", part_] = mark(v.tensor_reduce(mx[:, q], logits, AX, ALU.max))

            def centred(part_):
                q, logits, over_experts = part_of(part_)
                dv.wait_ge(s_v, wrote["largest", part_])
                v.tensor_tensor(sc[:, q, :], logits, over_experts(mx), ALU.subtract).then_inc(s_lmx, 1)
                v.tensor_copy(lg[:, q, :], logits)

            def summed(part_):
                q, logits, over_experts = part_of(part_)
                dv.wait_ge(s_gex, part_ + 1)
                wrote["summed", part_] = mark(v.tensor_reduce(mx[:, q], ex[:, q, :], AX, ALU.add))

            def inverted(part_):
                q, logits, over_experts = part_of(part_)
                dv.wait_ge(s_v, wrote["summed", part_])
                wrote["inverted", part_] = mark(v.reciprocal(inv[:, q], mx[:, q]))

            def divided(part_):
                q, logits, over_experts = part_of(part_)
                dv.wait_ge(s_v, wrote["inverted", part_])
                wrote["divided", part_] = mark(v.tensor_tensor(sc[:, q, :], ex[:, q, :], over_experts(inv), ALU.mult))

            def biased(part_):
                q, logits, over_experts = part_of(part_)
                dv.wait_ge(s_v, wrote["divided", part_])
                wrote["biased", part_] = mark(v.tensor_tensor(sc[:, q, :], sc[:, q, :],
                                                              over_tiles(bias[:], len(range(NT)[q])), ALU.add))

            def best(part_):
                dv.wait_ge(s_v, wrote["biased", part_])
                for t in range(NT)[part_of(part_)[0]]:
                    last = v.max(top[:, t, :], sc[:, t, :])
                wrote["best", part_] = mark(last)

            def picked(part_, tiles_):
                dv.wait_ge(s_v, wrote["best", part_])
                for t in tiles_:
                    last = v.max_index(pick[:, t, :], top[:, t, :], sc[:, t, :])
                return last

            largest(0), centred(0), summed(0), inverted(0), divided(0)
            largest(1), biased(0), centred(1), best(0)
            summed(1), picked(0, range(0, 4)), inverted(1), picked(0, range(4, 8)), divided(1)
            picked(0, range(8, 12)), biased(1), best(1)
            link(picked(1, range(12, 16)))
            dv.wait_ge(s_const, 16)
            eix = over_tiles(cst[:, C_EIX:C_EIX + E], NT)
            v.tensor_tensor(oh1[:], eix, pick[:, :, 0:1].broadcast_to([128, NT, E]), ALU.is_equal)
            link(v.tensor_tensor(oh2[:], eix, pick[:, :, 1:2].broadcast_to([128, NT, E]), ALU.is_equal))
            link(v.scalar_tensor_tensor(asg[:], oh1[:], -0.5, oh2[:], ALU.add, ALU.add))
            for rp in range(2):
                last = v.scalar_tensor_tensor(wmP[:, rp, :, :].rearrange("p e c -> p c e"), asg[:, rp::2, :], -2 * UNASSIGNED,
                                              lg[:, rp::2, :], ALU.mult, ALU.min)
            last.then_inc(s_wm, 1)
            v.tensor_tensor(oh1[:], oh1[:], lg[:], ALU.mult)
            weighed = mark(v.tensor_tensor(oh2[:], oh2[:], lg[:], ALU.mult))
            dv.wait_ge(s_kt, 1)
            by_token = "p (q rp r2) -> p rp r2 q"
            kt = bank[7][:, 0:CW]
            key_in = mark(v.tensor_scalar(K[:, :].rearrange(by_token, rp=2, r2=2),
                                          kt.rearrange("p (rp r2 q) -> p rp r2 q", rp=2, r2=2), 0.0, None, ALU.add))
            dv.wait_ge(s_v, weighed)
            v.tensor_reduce(h[:, :, D + 1], oh1[:], AX, ALU.add)
            dv.wait_ge(s_v, key_in)
            sign = mark(v.tensor_scalar(m32[:], K[:, :].bitcast(i32), 31, 2147483647, ALU.arith_shift_right, ALU.bitwise_and))
            v.tensor_reduce(h[:, :, D + 2], oh2[:], AX, ALU.add)
            dv.wait_ge(s_v, sign)
            ordered = mark(v.tensor_tensor(s32[:], K[:, :].bitcast(i32), m32[:], ALU.bitwise_xor))
            v.memset(h[:, :, D + 3], 0.0)
            v.tensor_copy(h[:, :, D], pick[:, :, 0]).then_inc(s_h1, 1)
            v.tensor_scalar(cand[:], cst[:, C_FIRST:C_FIRST + 3], 65536.0, -2147483648.0, ALU.mult, ALU.add)
            dv.wait_ge(s_v, ordered)
            upper = mark(v.tensor_scalar(part[:, 0], s32[:], -65536, None, ALU.bitwise_and))
            v.tensor_scalar(part[:, 1], s32[:], 65535, None, ALU.bitwise_and)
            dv.wait_ge(s_v, upper)
            link(v.tensor_copy(hi[:], part[:, 0]))

            start = done[0]
            per_round, between = 3, 6

            def search(half_, key, i, k):
                nth = half_ * ROUNDS + i * 4 + k
                steps = start + nth * per_round + half_ * between
                for m in range(3):
                    last = v.tensor_scalar(junk[:, m], key[:], cand[:, m:m + 1], None, ALU.is_ge, ALU.add,
                                           accum_out=cnt[:, m:m + 1])
                last.then_inc(s_cnt, 1)
                v.tensor_scalar(moves[:, :, 3], cst[:, bass.ds(C_CAND + 3 * nth, 3)], cand[:, 0:1], None,
                                ALU.add)
                v.tensor_copy(step[:], cst[:, bass.ds(C_STEP + nth, 1)]).then_inc(s_v, 1)
                dv.wait_ge(s_v, steps + 1)
                dv.wait_ge(s_tot, nth + 1)
                v.tensor_scalar(moves[:, :, 0:3], bank[6][:, 0:3].rearrange("p (o m) -> p o m", o=1).broadcast_to([128, 3, 3]),
                                float(CAP), step[:, 0:1], ALU.is_ge, ALU.mult).then_inc(s_v, 1)
                dv.wait_ge(s_v, steps + 2)
                v.tensor_reduce(cand[:], moves[:], AX, ALU.add).then_inc(s_v, 1)
                dv.wait_ge(s_v, steps + 3)

            with dv.Fori(0, 2) as i:
                for k in range(4):
                    search(0, hi, i, k)
            done[0] += ROUNDS * per_round
            dv.wait_ge(s_nct, 1)
            link(v.tensor_scalar(act[:], bank[6][:, 256:256 + E], 0.5 - N / 2, None, ALU.is_gt))
            v.tensor_tensor(used[:], act[:], cst[:, C_EIX:C_EIX + E], ALU.mult)
            ranked = mark(v.tensor_tensor_scan(rank[:], ones[:, 0:1].broadcast_to([128, E]), act[:], 0.0, ALU.mult, ALU.add))
            lower = mark(v.tensor_copy(lo[:], part[:, 1]))
            dv.wait_ge(s_v, ranked)
            placed = mark(v.scalar_tensor_tensor(at_place[:], rank[:], cst[:, C_PLACE:C_PLACE + 1], used[:], ALU.is_equal,
                                                 ALU.mult, accum_out=lval[:, 0:1]))
            dv.wait_ge(s_v, lower)
            based = mark(v.scalar_tensor_tensor(key2[:], hi[:], cand[:, 0:1], lo[:], ALU.subtract, ALU.add))
            dv.wait_ge(s_v, placed)
            v.tensor_scalar(lspread[:], cst[:, C_SPREAD:C_SPREAD + E], lval[:, 0:1], None, ALU.mult).then_inc(s_lval, 1)
            dv.wait_ge(s_v, based)
            first = mark(v.tensor_copy(cand[:], cst[:, C_FIRST:C_FIRST + 3]))
            v.tensor_scalar(assigned[:], K[:], UNASSIGNED / 2, None, ALU.is_gt)
            v.tensor_copy(R[:, CW:CW + 1], cst[:, C_CBASE:C_CBASE + 1])
            v.tensor_copy(elist_i[:, E:E + 1], rank[:, E - 1:E])
            dv.wait_ge(s_spread, 1)
            v.tensor_scalar(e320[:, 0:E], bank[6][:, 272:272 + E], float(CAP), None, ALU.mult)
            v.tensor_copy(elist[:], bank[6][:, 272:272 + E])
            v.tensor_copy(elist_i[:, 0:E], bank[6][:, 272:272 + E]).then_inc(s_list, 1)
            dv.wait_ge(s_v, first)
            assert done[0] == start + ROUNDS * per_round + between
            with dv.Fori(0, 2) as i:
                for k in range(4):
                    search(1, key2, i, k)
            done[0] += ROUNDS * per_round
            v.tensor_scalar(above[:], key2[:], cand[:, 0:1], None, ALU.is_gt, ALU.add, accum_out=tot[:, 0:1])
            v.scalar_tensor_tensor(ties[:], key2[:], cand[:, 0:1], assigned[:], ALU.is_equal, ALU.mult,
                                   accum_out=tot[:, 1:2]).then_inc(s_eq, 1)
            dv.wait_ge(s_eq, 1)
            one = ones[:, 0:1].broadcast_to([128, CW])
            v.tensor_tensor_scan(aboves[:], one, above[:], 0.0, ALU.mult, ALU.add)
            link(v.tensor_tensor_scan(tied[:], one, ties[:], 0.0, ALU.mult, ALU.add))
            dv.wait_ge(s_eqt, 1)
            v.tensor_scalar(rem[:], bank[6][:, 0:1], -1.0, float(CAP), ALU.mult, ALU.add)
            link(v.tensor_copy(offs[:], bank[6][:, 2:4]))
            v.tensor_scalar(off[:], offs[:, 1:2], rem[:, 0:1], offs[:, 0:1], ALU.min, ALU.add)
            link(v.tensor_scalar(tied[:], tied[:], offs[:, 1:2], rem[:, 0:1], ALU.add, ALU.min))
            v.scalar_tensor_tensor(R[:, 0:CW], aboves[:], offs[:, 0:1], tied[:], ALU.add, ALU.add).then_inc(s_R, 1)
            link(v.tensor_tensor(gstart[:], off[:], cst[:, C_GBASE:C_GBASE + 1], ALU.add))
            dv.wait_ge(s_list, 1)

            def compare(j, k):
                dv.wait_ge(s_G, j - 1 + START)
                v.tensor_scalar(ge[:, k], cst[:, C_IOTA:C_IOTA + 384], of_slot(e320, j), gstart[:, 0:1],
                                ALU.add, ALU.is_ge).then_inc(s_ge, 1)

            def tokens(j, k):
                dv.wait_ge(s_G, j + 1 + START)
                dv.wait_ge(s_tok, j + START)
                for m in range(3):
                    prefix = bank[P_BANK[k][m]]
                    last = v.tensor_scalar(junk[:, m], prefix[:, 0:CW], cst[:, C_SLOT + m:C_SLOT + m + 1],
                                           prefix[:, CW:CW + 1], ALU.is_le, ALU.add,
                                           accum_out=tokf[:, bass.ds(3 * j + m, 1)])
                last.then_inc(s_tok, 1)

            compare(0, 0)
            dv.wait_ge(s_D, 1)
            v.tensor_copy(Dl[:], bank[5][:, 0:CW + 1]).then_inc(s_Dc, 1)
            compare(1, 1)
            n = in_use(dv)

            def tokens_and_compare(j, k):
                tokens(j, k % 2)
                with dv.If(j + 2 < n):
                    compare(j + 2, k % 2)

            tokens_and_compare(0, 0), tokens_and_compare(1, 1)
            places(dv, n, tokens_and_compare, 2)
            steps = done[0]

            def expert(j, k):
                dv.wait_ge(s_gat[k], loaded(j, k))
                v.tensor_scalar(ne1[:, k], xg[:, k, :, D], of_slot(elist, j), None, ALU.not_equal)
                v.tensor_tensor(wdiff[:, k], xg[:, k, :, D + 2], xg[:, k, :, D + 1], ALU.subtract).then_inc(s_v, 3)
                dv.wait_ge(s_v, steps + 6 * j + 3)
                v.tensor_tensor(wdiff[:, k], wdiff[:, k], ne1[:, k], ALU.mult).then_inc(s_v, 3)
                dv.wait_ge(s_v, steps + 6 * j + 6)
                dv.wait_ge(s_yc, j + 1 - AHEAD + START)
                v.tensor_tensor(wslot[:, k], wdiff[:, k], xg[:, k, :, D + 1], ALU.add)
                dv.wait_ge(s_sct[k % 2], 24 * (j - k % 2) + 48 - 24 * AHEAD + ZEROED)
                dv.wait_ge(s_tok, n + START)
                v.scalar_tensor_tensor(dst[:, k], ne1[:, k], float(N), tokf[:, bass.ds(3 * j, 3)],
                                       ALU.mult, ALU.add).then_inc(s_dst, 1)
                for hb in range(HB):
                    dv.wait_ge(s_es, 2 * j + hb + 1)
                    v.tensor_tensor(gue[:, hb], sile[:, hb], bank[U_BANK[hb]][:, 0:CAP], ALU.mult).then_inc(s_eg, 1)

            places(dv, n, expert)
            def end_stats(b):
                dv.wait_ge(s_sum, b + 1)
                stats(3, b, lambda i, t: bank[SUM_BANK[b]][:, 128 * i:128 * i + 128])

            def residual(b):
                q = group(b, True)
                dv.wait_ge(s_n4, b + 1)
                v.tensor_tensor(res[:, q, :], total[:, q, :], x1[:, q, :], ALU.add).then_inc(s_fin, 1)

            end_stats(0), end_stats(1)
            q = group(B - 1, True)
            dv.wait_ge(s_yl[1], 32)
            v.tensor_tensor(y[:, q, :], y[:, q, :], y[:, NT + q.start:NT + q.stop:2, :], ALU.add).then_inc(s_y3, 1)
            end_stats(2), end_stats(3), residual(0), residual(1)
            dv.wait_ge(s_r[3], 3 * B - 2)
            for i, t in enumerate(group_tiles(B - 1, True)):
                v.scalar_tensor_tensor(total[:, t, :], bank[SUM_BANK[B - 1]][:, 128 * i:128 * i + 128],
                                       rstd[3][:, t:t + 1], x1[:, t, :], ALU.mult, ALU.add).then_inc(s_last, 1)
            residual(2)

        @block.tensor
        def _(pe):
            t_ = nc.tensor

            def keep_clock(bank_, times):
                for _i in range(times):
                    t_.matmul(bank[bank_][:], idle[:, 0:128], idle[:], start=True, stop=True)

            def transpose_x(b):
                pe.wait_ge(s_xn, b + 1) if b < BY_SCALAR else pe.wait_ge(s_xnv, b + 1 - BY_SCALAR)
                if b == 0:
                    pe.wait_ge(s_id, 16)
                else:
                    pe.wait_ge(s_xtc, max(b - 1, 1)) if b >= 2 else None
                for t in range(4):
                    last = t_.transpose(bank[b % 2][:, 128 * t:128 * t + 128], xn[:, 4 * b + t, 0:D], ident)
                last.then_inc(s_xt, 1)

            def scores(b):
                pe.wait_ge(s_xtc, b + 1)
                if b >= 2:
                    pe.wait_ge(s_ex, 2 * (b - 1))
                for t in range(4):
                    xt = xnT[:, 4 * b + t, :]
                    last = t_.matmul(bank[2 + b % 2][:, 128 * t:128 * t + 128], xt, xt, start=True, stop=True)
                last.then_inc(s_sc, 1)

            def attend(b):
                pe.wait_ge(s_ex, 2 * (b + 1))
                if b >= 2:
                    pe.wait_ge(s_x1, b - 1)
                for t in range(4 * b, 4 * b + 4):
                    last = t_.matmul(attended(t), P[:, t, :], xn[:, t, :], start=True, stop=True)
                last.then_inc(s_pv, 1)

            def transpose_h(b):
                pe.wait_ge(s_h, b + 1) if b < B - 1 else pe.wait_ge(s_hv, 1)
                pe.wait_ge(s_htc, b - 1) if b >= 2 else pe.wait_ge(s_xtc, b + 3)
                for t in range(4):
                    last = t_.transpose(bank[b % 2][:, 128 * t:128 * t + 128], h[:, 4 * b + t, 0:D], ident)
                last.then_inc(s_ht, 1)

            def gate(b):
                pe.wait_ge(s_htc, b + 1)
                part_ = b // 3
                for t in range(4 * b, 4 * b + 4):
                    at = E * (t - 4 * GATE_PARTS[part_][0])
                    last = t_.matmul(bank[GATE_BANK[part_]][:, at:at + E], hT[:, 128 * t:128 * t + 128], gw[:],
                                     start=True, stop=True)
                last.then_inc(s_lg, 1)

            pe.wait_ge(s_idle, 1)
            with pe.Fori(0, 7):
                keep_clock(7, 4)
            transpose_x(0), transpose_x(1), scores(0), scores(1), attend(0), transpose_x(2)
            attend(1), transpose_x(3), scores(2), scores(3)
            keep_clock(0, 4)
            attend(2)
            keep_clock(0, 14)
            attend(3)
            keep_clock(3, 4)
            pe.wait_ge(s_w, 64)
            for b in range(B):
                transpose_h(b)
                keep_clock(3, 4 if b < 2 else 2)
                gate(b)
                if b < 2:
                    keep_clock(3, 6 - 3 * b)

            def up(c, k):
                sh, hb = k // HB, k % HB
                xt = hT[:, bass.ds(c * 512, 512)]
                pe.wait_ge(s_sil, c * SU + k - 1 + START)
                t_.matmul(bank[SG_BANK[k % 2]][:], w1s[:, sh, 128 * hb:128 * hb + 128], xt, start=True, stop=True)
                t_.matmul(bank[SU_BANK[k % 2]][:], w3s[:, sh, 128 * hb:128 * hb + 128], xt,
                          start=True, stop=True).then_inc(s_up, 1)

            def totals(nth):
                pe.wait_ge(s_cnt, nth + 1)
                t_.matmul(bank[6][:, 0:3], blockb[:], cnt[:], start=True, stop=True).then_inc(s_tot, 1)

            def down(g, i):
                t = group_tiles(g, True)[i]
                for k in range(SU):
                    t_.matmul(bank[SUM_BANK[g]][:, 128 * i:128 * i + 128],
                              gu[:, SU * (t // 4) + k, 128 * (t % 4):128 * (t % 4) + 128],
                              w2m[:, k, :], start=i == 0 and k == 0, stop=False)

            up(0, 0), up(0, 1), up(0, 2)
            keep_clock(6, 4)
            pe.wait_ge(s_wm, 1)
            for rp in range(2):
                last = t_.transpose(bank[7][:, 128 * rp:128 * rp + 128],
                                    wmP[:, rp, :, :].rearrange("p e c -> p (e c)"), ident)
            last.then_inc(s_kt, 1)
            pe.wait_ge(s_set, 2)
            for t in range(NT):
                last = t_.matmul(bank[6][:, 256:256 + E], onesb[:], asg[:, t, :], start=t == 0, stop=t == NT - 1)
            last.then_inc(s_nct, 1)

            up(0, 3)
            keep_clock(2, 7)

            def rounds(i):
                for k in range(SU):
                    totals(4 * i + k)
                    up(i + 1, k)

            with pe.Fori(0, 2) as i:
                rounds(i)
            keep_clock(2, 2)
            pe.wait_ge(s_lval, 1)
            t_.matmul(bank[6][:, 272:272 + E], onesb[:], lspread[:], start=True, stop=True).then_inc(s_spread, 1)
            keep_clock(2, 5)
            rounds(2)
            for t in range(4):
                totals(12 + t)
                if t == 0:
                    pe.wait_ge(s_gu, 2 * SU + START)
                    pe.wait_ge(s_w2m, 1)
                    pe.wait_ge(s_sil, 4 * SU + START)
                down(0, t)
                keep_clock(0, 2)
            pe.wait_ge(s_eq, 1)
            t_.matmul(bank[6][:, 0:2], cst[:, C_BLOCK:C_BLOCK + 128], tot[:], start=True, stop=True)
            t_.matmul(bank[6][:, 2:4], beforef, tot[:], start=True, stop=True).then_inc(s_eqt, 1)
            down(2, 0), down(2, 1)
            n = in_use(pe)
            pe.wait_ge(s_R, 1)
            t_.matmul(bank[5][:, 0:CW + 1], deltah[:], R[:], start=True, stop=True).then_inc(s_D, 1)
            keep_clock(0, 2)
            pe.wait_ge(s_Dc, 1)

            def prefixes(j, k):
                pe.wait_ge(s_ge, j + 1)
                pe.wait_ge(s_tok, j - 1 + START)
                for m in range(3):
                    last = t_.matmul(bank[P_BANK[k % 2][m]][:, 0:CW + 1], ge[:, k % 2, 128 * m:128 * m + 128], Dl[:],
                                     start=True, stop=True)
                last.then_inc(s_G, 1)

            def prefixes_and_clock(j, k):
                prefixes(j, k)
                pe.wait_ge(s_tok, j + START)
                keep_clock(P_BANK[(k + 1) % 2][0], 4)

            prefixes(0, 0), down(2, 2)
            prefixes(1, 1), down(2, 3)
            places(pe, n, prefixes_and_clock, 2)

            def transpose_gathered(j, k):
                pe.wait_ge(s_gat[k], loaded(j, k))
                pe.wait_ge(s_gtc, j + START)
                for m, rows in enumerate(SLOT_ROWS):
                    last = t_.transpose(bank[0][:, 128 * m:128 * m + rows], xg[0:rows, k, m, 0:D],
                                        ident[0:rows, 0:rows])
                last.then_inc(s_gt, 1)

            def expert_up(j, k):
                pe.wait_ge(s_wl[k], loaded(j, k))
                pe.wait_ge(s_gtc, j + 1 + START)
                pe.wait_ge(s_eg, 2 * j + START)
                for hb in range(HB):
                    t_.matmul(bank[G_BANK[hb]][:, 0:CAP], w1e[:, k, 128 * hb:128 * hb + 128], xgT[:, k % 2], start=True, stop=True)
                    t_.matmul(bank[U_BANK[hb]][:, 0:CAP], w3e[:, k, 128 * hb:128 * hb + 128], xgT[:, k % 2],
                              start=True, stop=True).then_inc(s_eu, 1)

            def expert_down(j, k):
                pe.wait_ge(s_yc, j + START)
                for hb in range(HB):
                    pe.wait_ge(s_eg, 2 * j + hb + 1 + START)
                    for m in (0, 2, 1):
                        rows = SLOT_ROWS[m]
                        last = t_.matmul(bank[6][0:rows, 128 * m:128 * m + 128], gue[:, hb, 128 * m:128 * m + rows],
                                         w2e[:, k, hb, :], start=m == 0 and hb == 0, stop=m == 1 and hb == HB - 1)
                last.then_inc(s_ed, 1)

            pe.wait_ge(s_tok, n + START)
            transpose_gathered(0, 0)

            def expert(j, k):
                expert_up(j, k)
                with pe.If(j + 1 < n):
                    transpose_gathered(j + 1, (k + 1) % AHEAD)
                expert_down(j, k)

            places(pe, n, expert)
            pe.wait_ge(s_gu, 4 * SU + START)
            pe.wait_ge(s_eg, 2 * n + START)
            for g in (1, 3):
                for i in range(4):
                    down(g, i)
            keep_clock(2, 12)
            for g in range(B):
                choices = 2 if g < B - 1 else 1
                if g < B - 1:
                    pe.wait_ge(s_yl[g // 2], 32)
                else:
                    pe.wait_ge(s_y3, 1)
                for i, t in enumerate(group_tiles(g, True)):
                    for c in range(choices):
                        last = t_.matmul(bank[SUM_BANK[g]][:, 128 * i:128 * i + 128], ident, y[:, c * NT + t, :],
                                         start=False, stop=i == 3 and c == choices - 1)
                last.then_inc(s_sum, 1)


_INS = ["L0_attn_x", "L0_ffn_gate_w", "L0_ffn_gate_b", "L0_ffn_ew1", "L0_ffn_ew3", "L0_ffn_ew2",
        "L0_ffn_sw1", "L0_ffn_sw3", "L0_ffn_sw2"]


def kernel(**inputs):
    import numpy as _np
    import concourse.bacc as _bacc
    from concourse import mybir as _mybir
    from concourse.bass_utils import run_bass_kernel_spmd as _run

    nc = _bacc.Bacc("TRN2", target_bir_lowering=False, num_devices=1)
    arrays, args = {}, []
    for name in _INS:
        a = _np.ascontiguousarray(inputs[name])
        if name == "L0_attn_x":
            a = a.reshape(N, D)
        arrays[f"in_{name}"] = a
        args.append(nc.dram_tensor(f"in_{name}", a.shape, _mybir.dt.from_np(a.dtype), kind="ExternalInput").ap())
    arrays["in_constants"] = constants()
    args.append(nc.dram_tensor("in_constants", (128, C_ALL), _mybir.dt.float32, kind="ExternalInput").ap())
    args.append(nc.dram_tensor("out_0", (N, D), _mybir.dt.float32, kind="ExternalOutput").ap())
    build(nc, *args)
    r = _run(nc, [arrays], core_ids=[0])
    return r.results[0]["out_0"].reshape(B, T, D)
```
